# Optimizing a Trainium2 kernel written in Bass

```python
import numpy as np
import jax
import jax.numpy as jnp

def _softmax(x, axis=-1):
    return jax.nn.softmax(x, axis=axis)

def _gelu(x):
    return jax.nn.gelu(x, approximate=True)

def _silu(x):
    return jax.nn.silu(x)

def _sigmoid(x):
    return jax.nn.sigmoid(x)

def _layernorm(x, axis=-1, eps=1e-05):
    m = jnp.mean(x, axis=axis, keepdims=True)
    v = jnp.var(x, axis=axis, keepdims=True)
    return (x - m) / jnp.sqrt(v + eps)

def _scatter_add(tgt, idx, src, axis=0):
    return tgt.at[idx].add(src)

def _segment_sum(src, seg, n):
    return jax.ops.segment_sum(src, seg, n)
kernel_name = 'mk_macaron_d2_jaxref_r4_e44e8f'

def setup_inputs(seed: int=0):
    np.random.seed(seed)
    _w = jnp.asarray

    def _L0_attn_setup():
        import jax, jax.numpy as jnp
        import numpy as np
        NUM_HEADS = 16
        key = jax.random.key(seed)
        ks = jax.random.split(key, 6)
        B, S, D = (2, 512, 256)
        x = jax.random.normal(ks[0], (B, S, D), dtype=jnp.float32)
        s = 1.0 / np.sqrt(D)
        Wq = jax.random.normal(ks[1], (D, D), dtype=jnp.float32) * s
        Wk = jax.random.normal(ks[2], (D, D), dtype=jnp.float32) * s
        Wv = jax.random.normal(ks[3], (D, D), dtype=jnp.float32) * s
        Wff = jax.random.normal(ks[4], (D, D), dtype=jnp.float32) * s
        bff = jax.random.normal(ks[5], (D,), dtype=jnp.float32) * 0.01
        return {'x': x, 'Wq': Wq, 'Wk': Wk, 'Wv': Wv, 'Wff': Wff, 'bff': bff}
    _L0_attn_in = _L0_attn_setup()

    def _L0_ffn_setup():
        import jax, jax.numpy as jnp
        import numpy as np
        DIM = 256
        MOE_INTER = 256
        SHARED_INTER = 256
        N_EXPERTS = 6
        TOP_K = 2
        ROUTE_SCALE = 1.0
        B, S = (8, 1024)
        STD = 0.02 / np.sqrt(DIM)
        STD_I = 0.02 / np.sqrt(MOE_INTER)
        key = jax.random.key(seed)
        ks = jax.random.split(key, 10)
        inp = {'x': jax.random.normal(ks[0], (B, S, DIM), dtype=jnp.float32), 'gate_w': jax.random.normal(ks[1], (N_EXPERTS, DIM), dtype=jnp.float32) * STD, 'gate_b': jnp.zeros((N_EXPERTS,), dtype=jnp.float32), 'ew1': jax.random.normal(ks[2], (N_EXPERTS, MOE_INTER, DIM), dtype=jnp.float32) * STD, 'ew2': jax.random.normal(ks[3], (N_EXPERTS, DIM, MOE_INTER), dtype=jnp.float32) * STD_I, 'ew3': jax.random.normal(ks[4], (N_EXPERTS, MOE_INTER, DIM), dtype=jnp.float32) * STD, 'fc1': jax.random.normal(ks[5], (SHARED_INTER, DIM), dtype=jnp.float32) * STD, 'fc2': jax.random.normal(ks[6], (SHARED_INTER, DIM), dtype=jnp.float32) * STD, 'fc3': jax.random.normal(ks[7], (DIM, SHARED_INTER), dtype=jnp.float32) * STD_I}
        return inp
    _L0_ffn_in = _L0_ffn_setup()

    def _L1_attn_setup():
        import jax, jax.numpy as jnp
        import numpy as np
        from math import sqrt
        HEADS = 16
        MODEL_DIM = 256
        DIM_PER_HEAD = MODEL_DIM // HEADS
        MAX_REL_POS = 32
        ROPE_BASE = 10000.0
        NEG_INF = -1e+18

        def _rope_cos_sin(seq_len, dim):
            inv_freq = 1.0 / ROPE_BASE ** (jnp.arange(0, dim, 2, dtype=jnp.float32) / dim)
            t = jnp.arange(seq_len, dtype=jnp.float32)
            ang = jnp.outer(t, inv_freq)
            return (jnp.cos(ang), jnp.sin(ang))

        def _apply_rotary_interleave(x, cos, sin):
            B, H, L, D = x.shape
            x_ = x.reshape(B, H, L, D // 2, 2)
            xe, xo = (x_[..., 0], x_[..., 1])
            c = cos[None, None, :, :]
            s = sin[None, None, :, :]
            oe = xe * c - xo * s
            oo = xe * s + xo * c
            return jnp.stack([oe, oo], axis=-1).reshape(B, H, L, D)
        key = jax.random.key(seed)
        ks = jax.random.split(key, 6)
        B, L = (2, 256)
        scale = 0.02
        x = jax.random.normal(ks[0], (B, L, MODEL_DIM), dtype=jnp.float32)
        w_q = jax.random.normal(ks[1], (MODEL_DIM, MODEL_DIM), dtype=jnp.float32) * scale
        w_k = jax.random.normal(ks[2], (MODEL_DIM, MODEL_DIM), dtype=jnp.float32) * scale
        w_v = jax.random.normal(ks[3], (MODEL_DIM, MODEL_DIM), dtype=jnp.float32) * scale
        w_o = jax.random.normal(ks[4], (MODEL_DIM, MODEL_DIM), dtype=jnp.float32) * scale
        rel_emb = jax.random.normal(ks[5], (2 * MAX_REL_POS + 1, DIM_PER_HEAD), dtype=jnp.float32) * scale
        return {'x': x, 'w_q': w_q, 'w_k': w_k, 'w_v': w_v, 'w_o': w_o, 'rel_emb': rel_emb}
    _L1_attn_in = _L1_attn_setup()

    def _L1_ffn_setup():
        import jax, jax.numpy as jnp
        import numpy as np
        from jax import lax
        T, B, I, M, O = (64, 64, 256, 256, 256)

        def _xavier(key, shape):
            fan_out, fan_in = shape
            limit = float(np.sqrt(6.0 / (fan_in + fan_out)))
            return jax.random.uniform(key, shape, jnp.float32, -limit, limit)
        key = jax.random.key(seed)
        ks = jax.random.split(key, 9)
        x = jax.random.normal(ks[0], (T, B, I), jnp.float32)
        return {'x': x, 'wf': _xavier(ks[1], (M, I)), 'uf': _xavier(ks[2], (M, M)), 'bf': jnp.zeros((M,), jnp.float32), 'wi': _xavier(ks[3], (M, I)), 'ui': _xavier(ks[4], (M, M)), 'bi': jnp.zeros((M,), jnp.float32), 'wc': _xavier(ks[5], (M, I)), 'uc': _xavier(ks[6], (M, M)), 'bc': jnp.zeros((M,), jnp.float32), 'wo': _xavier(ks[7], (O, I)), 'uo': _xavier(ks[8], (O, M)), 'bo': jnp.zeros((O,), jnp.float32), 'in_c': jnp.zeros((M,), jnp.float32)}
    _L1_ffn_in = _L1_ffn_setup()
    _d = {'L0_attn_x': _L0_attn_in['x'], 'L0_attn_Wq': _L0_attn_in['Wq'], 'L0_attn_Wk': _L0_attn_in['Wk'], 'L0_attn_Wv': _L0_attn_in['Wv'], 'L0_attn_Wff': _L0_attn_in['Wff'], 'L0_attn_bff': _L0_attn_in['bff'], 'L0_ffn_gate_w': _L0_ffn_in['gate_w'], 'L0_ffn_gate_b': _L0_ffn_in['gate_b'], 'L0_ffn_ew1': _L0_ffn_in['ew1'], 'L0_ffn_ew2': _L0_ffn_in['ew2'], 'L0_ffn_ew3': _L0_ffn_in['ew3'], 'L0_ffn_fc1': _L0_ffn_in['fc1'], 'L0_ffn_fc2': _L0_ffn_in['fc2'], 'L0_ffn_fc3': _L0_ffn_in['fc3'], 'L1_attn_w_q': _L1_attn_in['w_q'], 'L1_attn_w_k': _L1_attn_in['w_k'], 'L1_attn_w_v': _L1_attn_in['w_v'], 'L1_attn_w_o': _L1_attn_in['w_o'], 'L1_attn_rel_emb': _L1_attn_in['rel_emb'], 'L1_ffn_wf': _L1_ffn_in['wf'], 'L1_ffn_uf': _L1_ffn_in['uf'], 'L1_ffn_bf': _L1_ffn_in['bf'], 'L1_ffn_wi': _L1_ffn_in['wi'], 'L1_ffn_ui': _L1_ffn_in['ui'], 'L1_ffn_bi': _L1_ffn_in['bi'], 'L1_ffn_wc': _L1_ffn_in['wc'], 'L1_ffn_uc': _L1_ffn_in['uc'], 'L1_ffn_bc': _L1_ffn_in['bc'], 'L1_ffn_wo': _L1_ffn_in['wo'], 'L1_ffn_uo': _L1_ffn_in['uo'], 'L1_ffn_bo': _L1_ffn_in['bo'], 'L1_ffn_in_c': _L1_ffn_in['in_c']}
    _x0 = _d['L0_attn_x']
    _d['L0_attn_x'] = jax.random.normal(jax.random.fold_in(jax.random.key(seed), 1), (2, 2048, 256), dtype=_x0.dtype)
    del _x0
    return _d

def reference(L0_attn_x, L0_attn_Wq, L0_attn_Wk, L0_attn_Wv, L0_attn_Wff, L0_attn_bff, L0_ffn_gate_w, L0_ffn_gate_b, L0_ffn_ew1, L0_ffn_ew2, L0_ffn_ew3, L0_ffn_fc1, L0_ffn_fc2, L0_ffn_fc3, L1_attn_w_q, L1_attn_w_k, L1_attn_w_v, L1_attn_w_o, L1_attn_rel_emb, L1_ffn_wf, L1_ffn_uf, L1_ffn_bf, L1_ffn_wi, L1_ffn_ui, L1_ffn_bi, L1_ffn_wc, L1_ffn_uc, L1_ffn_bc, L1_ffn_wo, L1_ffn_uo, L1_ffn_bo, L1_ffn_in_c):

    def _L0_attn_ref(x, Wq, Wk, Wv, Wff, bff):
        import jax, jax.numpy as jnp
        import numpy as np
        NUM_HEADS = 16
        B, S, D = x.shape
        H = NUM_HEADS
        Dh = D // H
        q = x @ Wq.T * (1.0 / jnp.sqrt(jnp.asarray(D, x.dtype)))
        k = x @ Wk.T
        v = x @ Wv.T
        q = q.reshape(B, S, H, Dh)
        k = k.reshape(B, S, H, Dh)
        v = v.reshape(B, S, H, Dh)
        scores = jnp.einsum('bqhd,bkhd->bhqk', q, k)
        attn = jax.nn.softmax(scores, axis=-1)
        out = jnp.einsum('bhqk,bkhd->bqhd', attn, v).reshape(B, S, D)
        return out @ Wff.T + bff

    def _L0_ffn_ref(x, gate_w, gate_b, ew1, ew2, ew3, fc1, fc2, fc3):
        import jax, jax.numpy as jnp
        import numpy as np
        DIM = 256
        MOE_INTER = 256
        SHARED_INTER = 256
        N_EXPERTS = 6
        TOP_K = 2
        ROUTE_SCALE = 1.0
        B, S = (8, 1024)
        STD = 0.02 / np.sqrt(DIM)
        STD_I = 0.02 / np.sqrt(MOE_INTER)
        orig_shape = x.shape
        xt = x.reshape(-1, DIM)
        logits = xt @ gate_w.T + gate_b
        probs = jax.nn.sigmoid(logits)
        w, idx = jax.lax.top_k(probs, TOP_K)
        w = w / (jnp.sum(w, axis=-1, keepdims=True) + 1e-08)
        w = w * ROUTE_SCALE
        ge = jnp.sum(jax.nn.one_hot(idx, N_EXPERTS, dtype=w.dtype) * w[..., None], axis=1)
        y = jnp.zeros_like(xt)
        for e in range(N_EXPERTS):
            h = jax.nn.silu(xt @ ew1[e].T) * (xt @ ew3[e].T)
            y = y + ge[:, e:e + 1] * (h @ ew2[e].T)
        z = jax.nn.silu(xt @ fc1.T) * (xt @ fc2.T) @ fc3.T
        return (y + z).reshape(orig_shape)

    def _L1_attn_ref(x, w_q, w_k, w_v, w_o, rel_emb):
        import jax, jax.numpy as jnp
        import numpy as np
        from math import sqrt
        HEADS = 16
        MODEL_DIM = 256
        DIM_PER_HEAD = MODEL_DIM // HEADS
        MAX_REL_POS = 32
        ROPE_BASE = 10000.0
        NEG_INF = -1e+18

        def _rope_cos_sin(seq_len, dim):
            inv_freq = 1.0 / ROPE_BASE ** (jnp.arange(0, dim, 2, dtype=jnp.float32) / dim)
            t = jnp.arange(seq_len, dtype=jnp.float32)
            ang = jnp.outer(t, inv_freq)
            return (jnp.cos(ang), jnp.sin(ang))

        def _apply_rotary_interleave(x, cos, sin):
            B, H, L, D = x.shape
            x_ = x.reshape(B, H, L, D // 2, 2)
            xe, xo = (x_[..., 0], x_[..., 1])
            c = cos[None, None, :, :]
            s = sin[None, None, :, :]
            oe = xe * c - xo * s
            oo = xe * s + xo * c
            return jnp.stack([oe, oo], axis=-1).reshape(B, H, L, D)
        B, L, _ = x.shape

        def shape(t):
            return t.reshape(B, L, HEADS, DIM_PER_HEAD).transpose(0, 2, 1, 3)
        q = shape(x @ w_q.T)
        k = shape(x @ w_k.T)
        v = shape(x @ w_v.T)
        cos, sin = _rope_cos_sin(L, DIM_PER_HEAD)
        q = _apply_rotary_interleave(q, cos, sin)
        k = _apply_rotary_interleave(k, cos, sin)
        q = q / sqrt(DIM_PER_HEAD)
        scores = jnp.einsum('bhqd,bhkd->bhqk', q, k)
        pos = jnp.arange(L)
        rel_idx = jnp.clip(pos[None, :] - pos[:, None], -MAX_REL_POS, MAX_REL_POS) + MAX_REL_POS
        rel = rel_emb[rel_idx]
        scores = scores + jnp.einsum('bhqd,qkd->bhqk', q, rel)
        causal = jnp.tril(jnp.ones((L, L), dtype=bool))
        scores = jnp.where(causal[None, None], scores, NEG_INF)
        attn = jax.nn.softmax(scores, axis=-1)
        ctx = jnp.einsum('bhqk,bhkd->bhqd', attn, v)
        ctx = ctx + jnp.einsum('bhqk,qkd->bhqd', attn, rel)
        out = ctx.transpose(0, 2, 1, 3).reshape(B, L, MODEL_DIM) @ w_o.T
        return out

    def _L1_ffn_ref(x, wf, uf, bf, wi, ui, bi, wc, uc, bc, wo, uo, bo, in_c):
        import jax, jax.numpy as jnp
        import numpy as np
        from jax import lax
        T, B, I, M, O = (64, 64, 256, 256, 256)

        def _xavier(key, shape):
            fan_out, fan_in = shape
            limit = float(np.sqrt(6.0 / (fan_in + fan_out)))
            return jax.random.uniform(key, shape, jnp.float32, -limit, limit)
        batch = x.shape[1]
        c0 = jnp.broadcast_to(in_c, (batch, in_c.shape[0]))

        def step(c, xt):
            ft = jax.nn.sigmoid(xt @ wf.T + c @ uf.T + bf)
            it = jax.nn.sigmoid(xt @ wi.T + c @ ui.T + bi)
            gt = jnp.tanh(xt @ wc.T + c @ uc.T + bc)
            c = ft * c + it * gt
            return (c, None)
        c_final, _ = lax.scan(step, c0, x)
        h = jnp.tanh(jnp.einsum('tbi,oi->tbo', x, wo) + c_final @ uo.T + bo)
        return h
    x = L0_attn_x
    x = x + 0.5 * _L0_ffn_ref(_layernorm(x, axis=-1), L0_ffn_gate_w, L0_ffn_gate_b, L0_ffn_ew1, L0_ffn_ew2, L0_ffn_ew3, L0_ffn_fc1, L0_ffn_fc2, L0_ffn_fc3)
    x = x + _L0_attn_ref(_layernorm(x, axis=-1), L0_attn_Wq, L0_attn_Wk, L0_attn_Wv, L0_attn_Wff, L0_attn_bff)
    x = x + 0.5 * _L0_ffn_ref(_layernorm(x, axis=-1), L0_ffn_gate_w, L0_ffn_gate_b, L0_ffn_ew1, L0_ffn_ew2, L0_ffn_ew3, L0_ffn_fc1, L0_ffn_fc2, L0_ffn_fc3)
    x = x + 0.5 * _L1_ffn_ref(_layernorm(x, axis=-1), L1_ffn_wf, L1_ffn_uf, L1_ffn_bf, L1_ffn_wi, L1_ffn_ui, L1_ffn_bi, L1_ffn_wc, L1_ffn_uc, L1_ffn_bc, L1_ffn_wo, L1_ffn_uo, L1_ffn_bo, L1_ffn_in_c)
    x = x + _L1_attn_ref(_layernorm(x, axis=-1), L1_attn_w_q, L1_attn_w_k, L1_attn_w_v, L1_attn_w_o, L1_attn_rel_emb)
    x = x + 0.5 * _L1_ffn_ref(_layernorm(x, axis=-1), L1_ffn_wf, L1_ffn_uf, L1_ffn_bf, L1_ffn_wi, L1_ffn_ui, L1_ffn_bi, L1_ffn_wc, L1_ffn_uc, L1_ffn_bc, L1_ffn_wo, L1_ffn_uo, L1_ffn_bo, L1_ffn_in_c)
    return x

_drawn_inputs = setup_inputs


def setup_inputs(seed=0):
    import zlib

    import numpy as np

    out = dict(_drawn_inputs(seed))
    spreads = {'L0_ffn_gate_b': (0.0, 2.0),
     'L1_ffn_bf': (0.0, 0.8),
     'L1_ffn_bi': (0.0, 0.8),
     'L1_ffn_bc': (0.0, 0.1),
     'L1_ffn_bo': (0.0, 0.1),
     'L1_ffn_in_c': (0.0, 0.29)}
    factors = {'L0_attn_Wq': 3.245,
     'L0_attn_Wk': 3.157,
     'L0_attn_bff': 4.985,
     'L0_ffn_gate_w': 64.0,
     'L0_ffn_ew1': 64.0,
     'L0_ffn_ew2': 64.0,
     'L0_ffn_ew3': 64.0,
     'L0_ffn_fc1': 58.406,
     'L0_ffn_fc2': 58.364,
     'L0_ffn_fc3': 58.437,
     'L1_attn_w_q': 8.0,
     'L1_attn_w_k': 8.0,
     'L1_attn_w_v': 8.0,
     'L1_attn_w_o': 6.391,
     'L1_attn_rel_emb': 8.0,
     'L1_ffn_uf': 4.156}
    for name, (base, spread) in spreads.items():
        noise = np.random.default_rng([zlib.crc32(name.encode()), seed]).standard_normal(out[name].shape)
        drawn = base * np.exp(spread * noise) if base else spread * noise
        out[name] = jnp.asarray(drawn.astype(out[name].dtype))
    for name, factor in factors.items():
        out[name] = (out[name] * factor).astype(out[name].dtype)
    return out
```

```python
from contextlib import ExitStack

import numpy as np

import concourse.bass as bass
from concourse import mybir

ALU = mybir.AluOpType
ACT = mybir.ActivationFunctionType
F32 = mybir.dt.float32
BF16 = mybir.dt.bfloat16
AX_X = mybir.AxisListType.X

P = 128
D = 256
C = D // P
NB, S = 2, 2048
TOK = NB * S
TT = TOK // P
BLK = 512
TB = BLK // P
NBLK = TOK // BLK
TOP_K = 2
E = 6
H, DH = 16, 16
HC = P // DH
EPS = 1e-5


class Core:

    def __init__(self, nc, io):
        self.nc, self.io = nc, io
        self.taken = []

    def semaphore(self, name):
        s = self.nc.alloc_semaphore(name=name)
        self.taken.append(s)
        return s

    def free_semaphores(self):
        nums = sorted(s.num for s in self.taken)
        first = [n for n in nums if n - 1 not in nums]
        after = [n + 1 for n in nums if n + 1 not in nums]
        with self.nc.Block() as block:
            @block.sync
            def _(sp):
                for lo, hi in zip(first, after):
                    sp.sem_clear(range(lo, hi))
        for s in self.taken:
            self.nc.release_semaphore(s)
        self.taken = []


def alloc(nc, ctx, io):
    k = Core(nc, io)

    def sb(name, shape, dt=F32):
        return ctx.enter_context(nc.sbuf_tensor(name, shape, dt))

    k.X = sb("X", [P, TT, D])
    k.arena = sb("arena", [P, 21 * C * D])
    k.big = sb("big", [P, 19 * 1024])
    k.xn = sb("xn", [P, 2, TB, D])
    k.xT = sb("xT", [P, 2, C, BLK])
    k.st = sb("st", [P, 2, TB, 6])
    k.lnv = sb("lnv", [P, 2, 6, TB])
    k.ident = sb("ident_sb", [P, P])
    k.neghalf = sb("neghalf", [P, TB])
    k.psum = ctx.enter_context(nc.psum_tensor("psum", [P, 8, BLK], F32))
    return k


class LayerNorm:

    def __init__(self, k, sem):
        self.k = k
        self.dve = sem("ln_dve")
        self.var = sem("ln_var")
        self.rstd = sem("ln_rstd")
        self.xn = sem("ln_xn")
        self.DVE_STEPS = 3

    def dve_stats(self, dve, n, half, g):
        k, nc = self.k, self.k.nc
        base = n * self.DVE_STEPS
        st, v = k.st[:, half, :, :], k.lnv
        for t in range(TB):
            last = nc.vector.bn_stats(st[:, t, :], k.X[:, bass.ds(g + t, 1), :])
        last.then_inc(self.dve, 1)
        dve.wait_ge(self.dve, base + 1)
        nc.vector.tensor_tensor(v[:, half, 0, :], st[:, :, 1], st[:, :, 4], ALU.add)
        nc.vector.tensor_tensor(v[:, half, 1, :], st[:, :, 1], st[:, :, 4], ALU.subtract)
        nc.vector.tensor_tensor(v[:, half, 2, :], st[:, :, 2], st[:, :, 5], ALU.add).then_inc(self.dve, 1)
        dve.wait_ge(self.dve, base + 2)
        nc.vector.tensor_scalar(v[:, half, 0, :], v[:, half, 0, :], 0.5, None, ALU.mult)
        nc.vector.scalar_tensor_tensor(v[:, half, 3, :], v[:, half, 1, :], 0.25, v[:, half, 1, :],
                                       ALU.mult, ALU.mult)
        nc.vector.tensor_scalar(v[:, half, 2, :], v[:, half, 2, :], 1.0 / D, EPS,
                                ALU.mult, ALU.add).then_inc(self.dve, 1)
        dve.wait_ge(self.dve, base + 3)
        nc.vector.tensor_tensor(v[:, half, 4, :], v[:, half, 2, :], v[:, half, 3, :],
                                ALU.add).then_inc(self.var, 1)

    def pool_rstd(self, pool, n, half):
        k, nc = self.k, self.k.nc
        pool.wait_ge(self.var, n + 1)
        nc.gpsimd.tensor_tensor(k.lnv[:, half, 5, :], k.lnv[:, half, 4, :], k.neghalf[:, :],
                                ALU.pow).then_inc(self.rstd, 1)

    def dve_apply(self, dve, n, half, g):
        k, nc = self.k, self.k.nc
        dve.wait_ge(self.rstd, n + 1)
        for t in range(TB):
            last = nc.vector.tensor_scalar(k.xn[:, half, t, :], k.X[:, bass.ds(g + t, 1), :].rearrange("p a d -> p (a d)"),
                                           k.lnv[:, half, 0, t:t + 1], k.lnv[:, half, 5, t:t + 1],
                                           ALU.subtract, ALU.mult)
        last.then_inc(self.xn, 1)

    def pe_transpose(self, half, c, bank):
        k, nc = self.k, self.k.nc
        for t in range(TB):
            last = nc.tensor.transpose(k.psum[:, bank, t * P:(t + 1) * P],
                                       k.xn[:, half, t, c * P:(c + 1) * P], k.ident[:, :])
        return last


def looped(eng, blocks, body):
    with eng.Fori(0, blocks // 2 - 1) as it:
        for half in range(2):
            body(it * 2 + half, half, False)
    for half in range(2):
        body(blocks - 2 + half, half, half == 1)


def load_stage(k, ctx):
    nc, io = k.nc, k.io
    s_in = k.semaphore("s_in")
    with nc.Block() as block:
        @block.sync
        def _(sp):
            x_t = io["x"].rearrange("b (t p) d -> p (b t) d", p=P)
            for i in range(4):
                n = TT // 4
                sp.dma_start(k.X[:, i * n:(i + 1) * n, :], x_t[:, i * n:(i + 1) * n, :]).then_inc(s_in, 16)
            sp.dma_start(k.arena[:, :], io["moe_w"][:, :]).then_inc(s_in, 16)
            sp.dma_start(k.ident[:, :], io["ident"][:, :]).then_inc(s_in, 16)
            sp.wait_ge(s_in, 16 * 6)

        @block.vector
        def _(dve):
            nc.vector.memset(k.neghalf[:, :], -0.5)


def moe_stage(k, ctx, run):
    nc, io = k.nc, k.io
    sem = lambda name: k.semaphore(f"moe{run}_{name}")
    with ExitStack() as local:
        def sb(name, shape, dt=F32):
            return local.enter_context(nc.sbuf_tensor(f"moe{run}_{name}", shape, dt))

        W = k.arena[:, :].rearrange("p (e k c f) -> p e k c f", e=E + 1, k=3, c=C)
        big = k.big
        sg = big[:, 0:1024].rearrange("p (r n) -> p r n", r=2)
        ts = big[:, 1024:2048].rearrange("p (r n) -> p r n", r=2)
        h = big[:, 2048:4096].rearrange("p (r m n) -> p r m n", r=2, m=C)
        gwT = sb("gwT", [P, C, E])
        gb = sb("gb", [E, 1])
        pT = sb("pT", [P, 2, BLK])
        pr = sb("pr", [P, 2, TB, E])
        gt = sb("gt", [P, 2, TB, E, E])
        eq = sb("eq", [P, 2, TB, E, E])
        tie = sb("tie", [P, E * E])
        rank = sb("rank", [P, 2, TB, E])
        wsel = sb("wsel", [P, 2, TB, E])
        tot = sb("tot", [P, 2, TB])
        ge = sb("ge", [P, 2, TB, E])

        ln = LayerNorm(k, sem)
        s_w = sem("weights")
        s_zero = sem("zero")
        t_ready = sem("t_ready")
        t_free = sem("t_free")
        up_ready = sem("up_ready")
        sg_ready = sem("sg_ready")
        ts_ready = sem("ts_ready")
        h_ready = sem("h_ready")
        dn_ready = sem("dn_ready")
        x_upd = sem("x_upd")
        g_dve = sem("g_dve")
        g_tot = sem("g_tot")
        ge_ready = sem("ge_ready")
        U = C * (E + 1)
        CREDIT = 2

        with nc.Block() as block:
            @block.sync
            def _(sp):
                sp.wait_ge(s_zero, 1)
                sp.dma_start(gwT[:, :, :], io["gwT"][:, :, :]).then_inc(s_w, 16)
                sp.dma_start(gb[:, :], io["gb"][:, :]).then_inc(s_w, 16)
                sp.dma_start(tie[:, :], io["tie"][:, :]).then_inc(s_w, 16)

            @block.gpsimd
            def _(pool):
                nc.gpsimd.memset(pT[:, :, :], 0.0).then_inc(s_zero, 1)
                with pool.Fori(0, NBLK // 2) as it:
                    for half in range(2):
                        ln.pool_rstd(pool, it * 2 + half, half)

            @block.tensor
            def _(pe):
                def transpose(n, half, c):
                    if c == 0:
                        pe.wait_ge(ln.xn, n + 1)
                    pe.wait_ge(t_free, n * 4 + c + 1)
                    ln.pe_transpose(half, c, 6 + c).then_inc(t_ready, 1)

                def gate(n, half):
                    pe.wait_ge(t_free, n * 4 + 2 + CREDIT)
                    for c in range(C):
                        last = nc.tensor.matmul(k.psum[0:E, 6, :], gwT[:, c, :], k.xT[:, half, c, :],
                                                start=(c == 0), stop=(c == C - 1))
                    last.then_inc(t_ready, 1)

                def gate_transpose(n, half):
                    pe.wait_ge(t_free, n * 4 + 3 + CREDIT)
                    for t in range(TB):
                        last = nc.tensor.transpose(k.psum[:, 7, t * P:(t + 1) * P],
                                                   pT[:, half, t * P:(t + 1) * P], k.ident[:, :])
                    last.then_inc(t_ready, 1)

                def up(n, half, e):
                    for m in range(C):
                        u = 2 * e + m
                        pe.wait_ge(h_ready, n * U + u + 1)
                        for kind in range(2):
                            for c in range(C):
                                last = nc.tensor.matmul(k.psum[:, 2 * (u % 2) + kind, :],
                                                        W[:, e, kind, c, m * P:(m + 1) * P],
                                                        k.xT[:, half, c, :], start=(c == 0), stop=(c == C - 1))
                        last.then_inc(up_ready, 1)

                def down(n, e):
                    pe.wait_ge(h_ready, n * U + 2 * e + 2 + CREDIT)
                    for pair in range(2):
                        pe.wait_ge(x_upd, n * U + 2 * e + pair + 1)
                        for t2 in range(2):
                            t = 2 * pair + t2
                            for c in range(C):
                                last = nc.tensor.matmul(k.psum[:, 4 + pair, t2 * D:(t2 + 1) * D],
                                                        h[:, e % 2, c, t * P:(t + 1) * P], W[:, e, 2, c, :],
                                                        start=(c == 0), stop=(c == C - 1))
                        last.then_inc(dn_ready, 1)

                pe.wait_ge(s_w, 16 * 3)
                transpose(0, 0, 0)
                transpose(0, 0, 1)
                gate(0, 0)
                gate_transpose(0, 0)

                def blockwise(n, half, last):
                    up(n, half, 0)
                    for e in range(E + 1):
                        if e < E:
                            up(n, half, e + 1)
                        if not last:
                            if e == 3:
                                transpose(n + 1, 1 - half, 0)
                                transpose(n + 1, 1 - half, 1)
                            if e == 4:
                                gate(n + 1, 1 - half)
                            if e == 5:
                                gate_transpose(n + 1, 1 - half)
                        down(n, e)

                looped(pe, NBLK, blockwise)

            @block.scalar
            def _(act):
                act.sem_inc(t_free, CREDIT)

                def misc(n, half, i):
                    act.wait_ge(t_ready, n * 4 + i + 1)
                    if i < 2:
                        ins = nc.scalar.copy(k.xT[:, half, i, :], k.psum[:, 6 + i, :])
                    elif i == 2:
                        ins = nc.scalar.activation(pT[0:E, half, :], k.psum[0:E, 6, :], ACT.Sigmoid, bias=gb[:, 0:1])
                    else:
                        ins = nc.scalar.copy(pr[:, half, :, :], k.psum[:, 7, :].rearrange("p (t n) -> p t n", t=TB)[:, :, 0:E])
                    ins.then_inc(t_free, 1)

                act.wait_ge(s_w, 16 * 3)
                for i in range(4):
                    misc(0, 0, i)

                def blockwise(n, half, last):
                    for u in range(U):
                        act.wait_ge(up_ready, n * U + u + 1)
                        act.wait_ge(ts_ready, n * U + u + 1)
                        nc.scalar.activation(sg[:, u % 2, :], k.psum[:, 2 * (u % 2), :],
                                             ACT.Sigmoid).then_inc(sg_ready, 1)
                        if not last and u in (9, 10, 11, 12):
                            misc(n + 1, 1 - half, u - 9)

                looped(act, NBLK, blockwise)

            @block.vector
            def _(dve):
                dve.sem_inc(ts_ready, CREDIT)
                dve.sem_inc(h_ready, CREDIT)
                dve.sem_inc(x_upd, CREDIT)

                def gate(n, half):
                    base = n * 6
                    p = pr[:, half, :, :]
                    mine = p.unsqueeze(3).to_broadcast([P, TB, E, E])
                    other = p.unsqueeze(2).to_broadcast([P, TB, E, E])
                    dve.wait_ge(t_free, n * 4 + 4 + CREDIT)
                    nc.vector.tensor_tensor(gt[:, half], other, mine, ALU.is_gt)
                    nc.vector.tensor_tensor(eq[:, half], other, mine, ALU.is_equal).then_inc(g_dve, 1)
                    dve.wait_ge(g_dve, base + 1)
                    tie_b = tie[:, :].rearrange("p (e i) -> p e i", e=E).unsqueeze(1).to_broadcast([P, TB, E, E])
                    nc.vector.tensor_tensor(eq[:, half], eq[:, half], tie_b, ALU.mult).then_inc(g_dve, 1)
                    dve.wait_ge(g_dve, base + 2)
                    nc.vector.tensor_tensor(gt[:, half], gt[:, half], eq[:, half], ALU.add).then_inc(g_dve, 1)
                    dve.wait_ge(g_dve, base + 3)
                    nc.vector.reduce_sum(rank[:, half], gt[:, half], AX_X).then_inc(g_dve, 1)
                    dve.wait_ge(g_dve, base + 4)
                    nc.vector.scalar_tensor_tensor(wsel[:, half], rank[:, half], TOP_K - 0.5, p,
                                                   ALU.is_lt, ALU.mult).then_inc(g_dve, 1)
                    dve.wait_ge(g_dve, base + 5)
                    nc.vector.reduce_sum(tot[:, half], wsel[:, half], AX_X).then_inc(g_dve, 1)
                    dve.wait_ge(g_dve, base + 6)
                    nc.vector.tensor_scalar(tot[:, half], tot[:, half], 1e-8, None, ALU.add).then_inc(g_tot, 1)
                    dve.wait_ge(g_tot, n * 2 + 1)
                    nc.vector.reciprocal(tot[:, half], tot[:, half]).then_inc(g_tot, 1)
                    dve.wait_ge(g_tot, n * 2 + 2)
                    nc.vector.scalar_tensor_tensor(ge[:, half], wsel[:, half], 0.5,
                                                   tot[:, half].unsqueeze(2).to_broadcast([P, TB, E]),
                                                   ALU.mult, ALU.mult).then_inc(ge_ready, 1)

                def hidden(n, e):
                    for m in range(C):
                        u = 2 * e + m
                        dve.wait_ge(sg_ready, n * U + u + 1)
                        nc.vector.tensor_tensor(ts[:, u % 2, :], k.psum[:, 2 * (u % 2), :], sg[:, u % 2, :],
                                                ALU.mult).then_inc(ts_ready, 1)
                        dve.wait_ge(ts_ready, n * U + u + 1 + CREDIT)
                        nc.vector.tensor_tensor(h[:, e % 2, m, :], k.psum[:, 2 * (u % 2) + 1, :], ts[:, u % 2, :],
                                                ALU.mult).then_inc(h_ready, 1)

                def update(n, half, e):
                    for pair in range(2):
                        d = 2 * e + pair
                        dve.wait_ge(dn_ready, n * U + d + 1)
                        dve.wait_ge(x_upd, n * U + d - 1 + CREDIT)
                        for t2 in range(2):
                            t = 2 * pair + t2
                            xt = k.X[:, bass.ds(n * TB + t, 1), :].rearrange("p a d -> p (a d)")
                            w = ge[:, half, t, e:e + 1] if e < E else 0.5
                            last = nc.vector.scalar_tensor_tensor(xt, k.psum[:, 4 + pair, t2 * D:(t2 + 1) * D], w, xt,
                                                                  ALU.mult, ALU.add)
                        last.then_inc(x_upd, 1)

                ln.dve_stats(dve, 0, 0, 0)
                ln.dve_apply(dve, 0, 0, 0)
                dve.wait_ge(s_w, 16 * 3)
                gate(0, 0)

                def blockwise(n, half, last):
                    hidden(n, 0)
                    if not last:
                        ln.dve_stats(dve, n + 1, 1 - half, (n + 1) * TB)
                    dve.wait_ge(ge_ready, n + 1)
                    for e in range(E + 1):
                        if e < E:
                            hidden(n, e + 1)
                        if e == 1 and not last:
                            ln.dve_apply(dve, n + 1, 1 - half, (n + 1) * TB)
                        update(n, half, e)
                        if e == E - 1 and not last:
                            gate(n + 1, 1 - half)

                looped(dve, NBLK, blockwise)


NH = NB * H
KT = S // P
QB = S // BLK
RANK = 3
REL = 32
BAND = REL + P
SKEW = BAND + 1
NEG = -1e18
GROUP = 4
ROW = 6 * DH
VW = DH + 1
VP = 32


def heads_loop(eng, body):
    with eng.Fori(0, NH // 4 - 1) as it:
        for q in range(4):
            body(it * 4 + q, q, False)
    for q in range(4):
        body(NH - 4 + q, q, q == 3)


def batch(n):
    return n // (NBLK // NB)


def within(n):
    return n % (NBLK // NB)


def dram(k, name, shape, dt=F32):
    return k.nc.dram_tensor(name, shape, dt, kind="Internal").ap()


def alloc_attention(k, ctx):
    k.V = ctx.enter_context(k.nc.sbuf_tensor("values", [P, NB, H, KT, DH], F32))
    k.QD = [dram(k, f"qk_parts{m}", (RANK, NH * DH, S), BF16) for m in range(2)]
    k.ND = dram(k, "out_heads", (NH * DH, S))
    k.DD = dram(k, "denominators", (NH, S))
    k.RD = dram(k, "reciprocals", (NH, S))
    k.TD = dram(k, "rel_scores", (NH, KT, P, REL))
    k.BB = dram(k, "bias_tiles", (4, KT * P * SKEW + SKEW))
    k.PB = dram(k, "band_probs", (NH * KT, P * SKEW + 4))


def qkv_stage(k, ctx, causal):
    nc, io = k.nc, k.io
    L = int(causal)
    sem = lambda name: k.semaphore(f"qkv{L}_{name}")
    nw = 6 if causal else 4
    big = k.big
    at = [0]

    def take(n):
        at[0] += n
        return big[:, at[0] - n:at[0]]

    w = take(nw * C * D).rearrange("p (k c f) -> p k c f", k=nw, c=C)
    rr = take(2 * BLK).rearrange("p (r n) -> p r n", r=2)
    r1 = take(2 * BLK).rearrange("p (r n) -> p r n", r=2)
    parts = take(2 * RANK * BLK // 2).bitcast(BF16).rearrange("p (r t n) -> p r t n", r=2, t=RANK)
    if causal:
        cs = take(2 * S).rearrange("p (k n) -> p k n", k=2)
        ra = take(2 * BLK).rearrange("p (r n) -> p r n", r=2)
        rb = take(2 * BLK).rearrange("p (r n) -> p r n", r=2)
        relt = take(1 + REL)
        rel0, rel = relt[:, 0:1], relt[:, 1:]
        rel0row = take(D)
        hmask = take(HC)
        dbig = take(HC * REL)
        tsb = take(2 * TB * D).rearrange("p (r t n) -> p r t n", r=2, t=TB)
    ln = LayerNorm(k, sem)
    s_w = sem("weights")
    t_ready, t_free = sem("t_ready"), sem("t_free")
    u_ready = sem("u_ready")
    rr_ready = sem("rr_ready")
    p1_ready = sem("p1_ready")
    r1_ready = sem("r1_ready")
    p2_ready = sem("p2_ready")
    p3_ready = sem("p3_ready")
    s_parts = [sem(f"parts{r}") for r in range(2)]
    v_ready, v_free = sem("v_ready"), sem("v_free")
    rot = sem("rot")
    s_rel = sem("rel")
    s_t = [sem(f"t_stored{r}") for r in range(2)]
    CREDIT = 2
    NU = 4
    NV = 6 if causal else 2

    W_DMAS = 5 if causal else 1

    with nc.Block() as block:
        @block.sync
        def _(sp):
            name = f"attn{L}_w"
            sp.dma_start(big[:, 0:nw * C * D], io[name][:, :]).then_inc(s_w, 16)
            if causal:
                sp.dma_start(cs[:, :, :], io["rope"][:, :, :]).then_inc(s_w, 16)
                sp.dma_start(hmask, io["hmask"][:, :]).then_inc(s_w, 16)
                sp.dma_start(relt, io["relT"][:, :]).then_inc(s_w, 16)
                row = io["rel"][0:1, :].rearrange("a d -> (a d)").unsqueeze(0).unsqueeze(0).to_broadcast([P, H, DH])
                sp.dma_start(rel0row.rearrange("p (h d) -> p h d", h=H), row).then_inc(s_w, 16)

            def store(n, u):
                kind, m, r = u // C, u % C, u % 2
                sp.wait_ge(p3_ready, n * NU + u + 1)
                dst = k.QD[kind][:, bass.ds(batch(n) * D + m * P, P), bass.ds(within(n) * BLK, BLK)]
                sp.dma_start(dst.rearrange("t p c -> p t c"), parts[:, r, :, :]).then_inc(s_parts[r], 16)

            def store_t(n, m):
                sp.wait_ge(v_free, n * NV + 2 + 2 * (m + 1) + CREDIT)
                for t in range(TB):
                    dst = k.TD[bass.ds(batch(n) * H + m * HC, HC), bass.ds(within(n) * TB + t, 1), :, :]
                    sp.dma_start(dst.rearrange("h a p j -> p (h a) j"), tsb[:, m, t, :].rearrange("p (h j) -> p h j", h=HC)).then_inc(s_t[m], 16)

            for s in s_parts + s_t:
                sp.sem_inc(s, 16)
            with sp.Fori(0, NBLK) as n:
                for u in range(NU):
                    store(n, u)
                    if causal and u < C:
                        store_t(n, u)
            for r in range(2):
                sp.wait_ge(s_parts[r], 16 * (1 + NBLK * NU // 2))
                if causal:
                    sp.wait_ge(s_t[r], 16 * (1 + NBLK * TB))

        @block.gpsimd
        def _(pool):
            pool.sem_inc(r1_ready, CREDIT)

            def blockwise(n, half, last):
                for u in range(NU):
                    r = u % 2
                    if u == 1 and not last:
                        ln.pool_rstd(pool, n + 1, 1 - half)
                    pool.wait_ge(p1_ready, n * NU + u + 1)
                    nc.gpsimd.tensor_tensor(r1[:, r, :], rr[:, r, :], parts[:, r, 0, :], ALU.subtract).then_inc(r1_ready, 1)
                    pool.wait_ge(p2_ready, n * NU + u + 1)
                    nc.gpsimd.tensor_tensor(parts[:, r, 2, :], r1[:, r, :], parts[:, r, 1, :], ALU.subtract).then_inc(p3_ready, 1)

            ln.pool_rstd(pool, 0, 0)
            looped(pool, NBLK, blockwise)

        @block.tensor
        def _(pe):
            pe.wait_ge(s_w, 16 * W_DMAS)
            if causal:
                pe.wait_ge(s_rel, 2)

            def transpose(n, half, c):
                if c == 0:
                    pe.wait_ge(ln.xn, n + 1)
                pe.wait_ge(t_free, n * C + c + 1)
                ln.pe_transpose(half, c, 6 + c).then_inc(t_ready, 1)

            def unit(n, half, u):
                kind, m, r = u // C, u % C, u % 2
                pe.wait_ge(rr_ready, n * NU + u + 1)
                for s, which in enumerate((kind, 4 + kind) if causal else (kind,)):
                    for c in range(C):
                        last = nc.tensor.matmul(k.psum[:, 2 * r + s, :], w[:, which, c, m * P:(m + 1) * P],
                                                k.xT[:, half, c, :], start=(c == 0), stop=(c == C - 1))
                last.then_inc(u_ready, 1)

            def values(n, half, pair):
                pe.wait_ge(v_free, n * NV + pair + 1)
                for t2 in range(2):
                    t = 2 * pair + t2
                    for c in range(C):
                        last = nc.tensor.matmul(k.psum[:, 4 + pair, t2 * D:(t2 + 1) * D],
                                                k.xT[:, half, c, t * P:(t + 1) * P], w[:, 2, c, :],
                                                start=(c == 0), stop=(c == C - 1))
                last.then_inc(v_ready, 1)

            def band(n, m, pair):
                if pair == 0:
                    pe.wait_ge(rr_ready, n * NU + m + 1 + CREDIT)
                pe.wait_ge(v_free, n * NV + 2 + 2 * m + pair + 1)
                for t2 in range(2):
                    t = 2 * pair + t2
                    last = nc.tensor.matmul(k.psum[:, 4 + pair, t2 * D:(t2 + 1) * D],
                                            rr[:, m, t * P:(t + 1) * P], dbig, start=True, stop=True)
                last.then_inc(v_ready, 1)

            for c in range(C):
                transpose(0, 0, c)

            def blockwise(n, half, last):
                pe.wait_ge(t_free, n * C + C + CREDIT)
                unit(n, half, 0)
                unit(n, half, 1)
                for pair in range(2):
                    values(n, half, pair)
                if causal:
                    for m in range(C):
                        for pair in range(2):
                            band(n, m, pair)
                unit(n, half, 2)
                if not last:
                    for c in range(C):
                        transpose(n + 1, 1 - half, c)
                unit(n, half, 3)

            looped(pe, NBLK, blockwise)

        @block.scalar
        def _(act):
            act.sem_inc(t_free, CREDIT)
            if not causal:
                act.sem_inc(rr_ready, CREDIT)

            def chunk(n, half, c):
                act.wait_ge(t_ready, n * C + c + 1)
                nc.scalar.copy(k.xT[:, half, c, :], k.psum[:, 6 + c, :]).then_inc(t_free, 1)

            for c in range(C):
                chunk(0, 0, c)

            def blockwise(n, half, last):
                for u in range(NU):
                    r = u % 2
                    if not causal:
                        act.wait_ge(u_ready, n * NU + u + 1)
                        act.wait_ge(r1_ready, n * NU + u + 1)
                        nc.scalar.activation(rr[:, r, :], k.psum[:, 2 * r, :], ACT.Copy,
                                             scale=D ** -0.5 if u < C else 1.0).then_inc(rr_ready, 1)
                    act.wait_ge(rr_ready, n * NU + u + 1 + CREDIT)
                    act.wait_ge(s_parts[r], (n * 2 + u // 2 + 1) * 16)
                    nc.scalar.copy(parts[:, r, 0, :], rr[:, r, :]).then_inc(p1_ready, 1)
                    act.wait_ge(r1_ready, n * NU + u + 1 + CREDIT)
                    nc.scalar.copy(parts[:, r, 1, :], r1[:, r, :]).then_inc(p2_ready, 1)
                    if u >= 2 and not last:
                        chunk(n + 1, 1 - half, u - 2)

            looped(act, NBLK, blockwise)

        @block.vector
        def _(dve):
            dve.sem_inc(v_free, CREDIT)
            if causal:
                dve.sem_inc(rr_ready, CREDIT)
                dve.wait_ge(s_w, 16 * W_DMAS)
                nc.vector.tensor_scalar(rel, rel, rel0, None, ALU.subtract).then_inc(s_rel, 1)
                dve.wait_ge(s_rel, 1)
                nc.vector.tensor_tensor(dbig.rearrange("p (h j) -> p h j", h=HC),
                                        rel.unsqueeze(1).to_broadcast([P, HC, REL]),
                                        hmask.unsqueeze(2).to_broadcast([P, HC, REL]), ALU.mult).then_inc(s_rel, 1)
            ln.dve_stats(dve, 0, 0, 0)
            ln.dve_apply(dve, 0, 0, 0)

            def rotate(n, u):
                kind, r = u // C, u % 2
                cols = bass.ds(within(n) * BLK, BLK)
                scale = DH ** -0.5 if kind == 0 else 1.0
                dve.wait_ge(u_ready, n * NU + u + 1)
                dve.wait_ge(r1_ready, n * NU + u + 1)
                if u >= C:
                    dve.wait_ge(v_ready, n * NV + 2 + 2 * (u - C + 1))
                nc.vector.scalar_tensor_tensor(ra[:, r, :], k.psum[:, 2 * r, :], scale, cs[:, 0, cols],
                                               ALU.mult, ALU.mult)
                nc.vector.scalar_tensor_tensor(rb[:, r, :], k.psum[:, 2 * r + 1, :], scale, cs[:, 1, cols],
                                               ALU.mult, ALU.mult).then_inc(rot, 1)
                dve.wait_ge(rot, n * NU + u + 1)
                nc.vector.scalar_tensor_tensor(rr[:, r, :], ra[:, r, :], rel0 if kind else 0.0, rb[:, r, :],
                                               ALU.add, ALU.add).then_inc(rr_ready, 1)

            def values(n, pair):
                dve.wait_ge(v_ready, n * NV + pair + 1)
                src = k.psum[:, 4 + pair, :].rearrange("p (t h d) -> p t h d", t=2, h=H)
                for t2 in range(2):
                    dst = k.V[:, bass.ds(batch(n), 1), :, bass.ds(within(n) * TB + 2 * pair + t2, 1), :]
                    dst = dst.rearrange("p a h b d -> p (a h b) d")
                    if causal:
                        last = nc.vector.tensor_tensor(dst, src[:, t2], rel0row.rearrange("p (h d) -> p h d", h=H), ALU.add)
                    else:
                        last = nc.vector.tensor_copy(dst, src[:, t2])
                last.then_inc(v_free, 1)

            def band(n, m, pair):
                if pair == 0:
                    dve.wait_ge(s_t[m], (n * TB + 1) * 16)
                dve.wait_ge(v_ready, n * NV + 2 + 2 * m + pair + 1)
                nc.vector.tensor_copy(tsb[:, m, 2 * pair:2 * pair + 2, :],
                                      k.psum[:, 4 + pair, :].rearrange("p (t n) -> p t n", t=2)).then_inc(v_free, 1)

            def blockwise(n, half, last):
                if not last:
                    ln.dve_stats(dve, n + 1, 1 - half, (n + 1) * TB)
                if causal:
                    rotate(n, 0)
                    rotate(n, 1)
                for pair in range(2):
                    values(n, pair)
                if not last:
                    ln.dve_apply(dve, n + 1, 1 - half, (n + 1) * TB)
                if causal:
                    for m in range(C):
                        for pair in range(2):
                            band(n, m, pair)
                    rotate(n, 2)
                    rotate(n, 3)

            looped(dve, NBLK, blockwise)


def score_units(causal, kt):
    first = kt * P if causal else 0
    return [(j, max(first, j * BLK), (j + 1) * BLK) for j in range(QB) if (j + 1) * BLK > first]


def max_units(causal, t):
    wide = 2 * BLK
    end = t * P - REL if causal else S
    far = [("far", lo, min(lo + wide, end), lo // wide) for lo in range(0, max(end, 0), wide)]
    return far + [("band", t * P - REL, (t + 1) * P, 2)] * causal


def max_ring(causal):
    out = []
    for t in range(KT):
        out += [(t, u) + (t,) for u in max_units(causal, t)]
        if t % GROUP == 0 and t:
            out.append((t, ("row", t // GROUP - 1, 0, 0), t))
    out.append((KT - 1, ("row", KT // GROUP - 1, 0, 0), KT - 1))
    return out


def heads_stage(k, ctx, causal):
    nc, io = k.nc, k.io
    L = int(causal)
    sem = lambda name: k.semaphore(f"heads{L}_{name}")
    big = k.big
    at = [0]

    def take(n, dt=F32):
        at[0] += n
        v = big[:, at[0] - n:at[0]]
        return v.bitcast(dt) if dt != F32 else v

    q_sb = take(4 * S // 2, BF16).rearrange("p (r n) -> p r n", r=4)
    k_sb = take(4 * S // 2, BF16).rearrange("p (r n) -> p r n", r=4)
    pT = take(4 * S).rearrange("p (r n) -> p r n", r=4)
    vh = take(2 * KT * VP).rearrange("p (r t d) -> p r t d", r=2, t=KT)
    osb = take(2 * BLK).rearrange("p (r n) -> p r n", r=2)
    mx = take(2 * KT * 3).rearrange("p (r t s) -> p r t s", r=2, t=KT)
    mm = take(2 * KT).rearrange("p (r t) -> p r t", r=2)
    nm = take(2 * KT // 2, BF16).rearrange("p (r t) -> p r t", r=2)
    identb = take(P // 2, BF16)
    if causal:
        bt = k.arena[:, 0:4 * KT * BAND].rearrange("p (r t c) -> p r t c", r=4, t=KT)
        sb = [buf[:, :, :, :].rearrange("p a b c -> p (a b c)")[:, 0:KT // 2 * BAND].rearrange("p (t c) -> p t c", c=BAND)
              for buf in (k.xn, k.xT)]
        band_of = lambda t: sb[t // (KT // 2)][:, t % (KT // 2), :]

    SU = [score_units(causal, kt) for kt in range(KT)]
    S_BEFORE = [sum(len(x) for x in SU[:kt]) for kt in range(KT + 1)]
    NS = S_BEFORE[KT]
    RING = max_ring(causal)
    NM = len(RING)
    ROWS_AT = [n for n, (_, u, _) in enumerate(RING) if u[0] == "row"]
    LOADS = 6 + 3
    NG = KT // GROUP
    PVC = 4 * KT
    MC = 2
    assert NM % 2 == 0

    qk_loaded = [sem(f"qk_loaded{q}") for q in range(4)]
    bt_loaded = [sem(f"bt_loaded{q}") for q in range(4)]
    skewed = [sem(f"skewed{q}") for q in range(4)]
    prefilled = sem("prefilled")
    const = sem("const")
    s_ready = sem("s_ready")
    p_ready = sem("p_ready")
    pv_done = sem("pv_done")
    m_ready = sem("m_ready")
    m_free = sem("m_free")
    mm_ready = sem("mm_ready")
    nm_ready = sem("nm_ready")
    band_sum = sem("band_sum")
    pb_ready = sem("pb_ready")
    pb_stored = [sem(f"pb_stored{g}") for g in range(NG)]
    vh_ready = sem("vh_ready")
    o_free = sem("o_free")
    o_stored = [sem(f"o_stored{r}") for r in range(2)]

    def band_cols(t):
        return (REL if t == 0 else 0), BAND

    with nc.Block() as block:
        @block.sync
        def _(sp):
            def load(i, q, turn):
                sp.wait_ge(pv_done, i * KT + KT)
                rows = bass.ds(i * DH, DH)
                at = 0
                for part, n in ((0, 3), (1, 2), (2, 1)):
                    for _ in range(n):
                        sp.dma_start(q_sb[at:at + DH, q, :], k.QD[0][part, rows, :]).then_inc(qk_loaded[q], 16)
                        at += DH
                at = 0
                for n in (3, 2, 1):
                    sp.dma_start(k_sb[at:at + n * DH, q, :], k.QD[1][0:n, rows, :]).then_inc(qk_loaded[q], 16)
                    at += n * DH
                if causal:
                    diag = k.BB[q, 1:1 + KT * P * SKEW].rearrange("(r c) -> r c", c=SKEW)[:, 0:REL]
                    src = k.TD[bass.ds(i, 1), :, :, :].rearrange("a t r j -> (a t r) j")
                    sp.dma_start(diag, src).then_inc(skewed[q], 16)
                    sp.wait_ge(skewed[q], 16 * (turn + 1))
                    slot = k.BB[q, 0:KT * P * SKEW].rearrange("(t x) -> t x", t=KT)[:, 0:P * BAND]
                    sp.dma_start(bt[:, q, :, :], slot.rearrange("t (r c) -> r t c", c=BAND)).then_inc(bt_loaded[q], 16)

            def store(j, r):
                sp.wait_ge(o_free, j + 2)
                for b in range(QB):
                    cols = slice(b * BLK, (b + 1) * BLK)
                    sp.dma_start(k.ND[bass.ds(j * DH, DH), cols], osb[32 * b:32 * b + DH, r, :]).then_inc(o_stored[r], 16)
                    sp.dma_start(k.DD[bass.ds(j, 1), cols], osb[32 * b + DH:32 * b + VW, r, :]).then_inc(o_stored[r], 16)

            if causal:
                for q in range(4):
                    for t in range(KT):
                        dst = k.BB[q, t * P * SKEW:t * P * SKEW + P * BAND].rearrange("(r c) -> r c", c=BAND)
                        sp.dma_start(dst, io["bias0"][:, 0:BAND]).then_inc(prefilled, 16)
                sp.wait_ge(prefilled, 16 * 4 * KT)
            for r in range(2):
                sp.sem_inc(o_stored[r], 16)
            for q in range(4):
                load(q, q, 0)
            with sp.Fori(1, NH // 4) as it:
                for q in range(4):
                    load(it * 4 + q, q, it)
                    store((it - 1) * 4 + q, q % 2)
            for q in range(4):
                store(NH - 4 + q, q % 2)
            for r in range(2):
                sp.wait_ge(o_stored[r], 16 * (1 + 2 * QB * NH // 2))

        @block.gpsimd
        def _(pool):
            def store_band(i, g):
                pool.wait_ge(pb_ready, i * NG + g + 1)
                for t in range(g * GROUP, (g + 1) * GROUP):
                    dst = k.PB[bass.ds(i * KT + t, 1), 0:P * BAND].rearrange("a (r c) -> (a r) c", c=BAND)
                    pool.dma_start(dst, band_of(t)).then_inc(pb_stored[g], 16)

            def gather(i, q):
                pool.wait_ge(pv_done, PVC + (i - 1) * KT)
                src = k.V[:, bass.ds(i // H, 1), bass.ds(i % H, 1), :, :].rearrange("p a b t d -> p (a b t) d")
                nc.gpsimd.tensor_copy(vh[:, q % 2, :, 0:DH], src).then_inc(vh_ready, 1)

            pool.wait_ge(const, 1)
            if causal:
                for g in range(NG - 1):
                    store_band(0, g)

            def body(i, q, last):
                gather(i, q)
                if causal:
                    store_band(i, NG - 1)
                    if not last:
                        for g in range(NG - 1):
                            store_band(i + 1, g)

            heads_loop(pool, body)
            if causal:
                for g in range(NG):
                    pool.wait_ge(pb_stored[g], 16 * GROUP * NH)

        @block.tensor
        def _(pe):
            def scores(i, q, kt, n):
                u = S_BEFORE[kt] + n
                j, lo, hi = SU[kt][n]
                bank = 4 + u % 3
                if u >= 3:
                    pe.wait_ge(p_ready, NS + i * NS + u - 2)
                else:
                    former = max(v for v in range(NS) if v % 3 == u)
                    pe.wait_ge(p_ready, i * NS + former + 1)
                if kt == 0:
                    pe.wait_ge(m_free, MC + i * NM + ROWS_AT[j] + 1)
                last = nc.tensor.matmul(k.psum[:, bank, 0:hi - lo], k_sb[0:ROW + 1, q, kt * P:(kt + 1) * P],
                                        q_sb[0:ROW + 1, q, lo:hi], start=True, stop=not causal, skip_group_check=causal)
                if causal and lo <= kt * P < hi:
                    at = kt * P - lo
                    last = nc.tensor.matmul(k.psum[:, bank, at:at + P], bt[:, q, kt, REL:BAND], k.ident[:, :],
                                            start=False, stop=True, skip_group_check=True)
                if causal and lo <= (kt + 1) * P < hi:
                    at = (kt + 1) * P - lo
                    last = nc.tensor.matmul(k.psum[P - REL:P, bank, at:at + REL], bt[:, q, kt + 1, 0:REL],
                                            k.ident[:, 0:REL], start=False, stop=True, skip_group_check=True)
                last.then_inc(s_ready, 1)

            def weighted(i, q, kt):
                pe.wait_ge(p_ready, NS + i * NS + S_BEFORE[kt + 1])
                if kt == 0:
                    pe.wait_ge(vh_ready, i + 1)
                    pe.wait_ge(o_free, i + 1)
                for j, lo, hi in SU[kt]:
                    last = nc.tensor.matmul(k.psum[32 * j:32 * j + VP, 7, lo - j * BLK:hi - j * BLK],
                                            vh[:, q % 2, kt, :], pT[:, kt % 4, lo:hi],
                                            start=(kt == 0), stop=(kt == KT - 1), skip_group_check=True)
                last.then_inc(pv_done, 1)

            def maxima(i, q, idx):
                _, (kind, lo, hi, slot), t = RING[idx]
                b = 2 * (idx % 2)
                pe.wait_ge(m_free, i * NM + idx + 1)
                if kind == "far":
                    for c in range(lo, hi, BLK):
                        e = min(c + BLK, hi)
                        last = nc.tensor.matmul(k.psum[:, b + (c - lo) // BLK, 0:e - c],
                                                q_sb[0:ROW, q, t * P:(t + 1) * P], k_sb[0:ROW, q, c:e],
                                                start=True, stop=True)
                elif kind == "band":
                    c0, c1 = band_cols(t)
                    last = nc.tensor.matmul(k.psum[:, b, c0:c1], q_sb[0:ROW, q, t * P:(t + 1) * P],
                                            k_sb[0:ROW, q, lo + c0:hi], start=True, stop=True)
                else:
                    pe.wait_ge(nm_ready, i * NG + lo + 1)
                    for n in range(GROUP):
                        last = nc.tensor.matmul(k.psum[ROW:ROW + 1, b, n * P:(n + 1) * P],
                                                nm[:, q % 2, lo * GROUP + n:lo * GROUP + n + 1], identb[:, :],
                                                start=True, stop=True)
                last.then_inc(m_ready, 1)

            def arrived(i, q):
                pe.wait_ge(qk_loaded[q], 16 * LOADS * (i // 4 + 1))
                if causal:
                    pe.wait_ge(bt_loaded[q], 16 * (i // 4 + 1))

            pe.wait_ge(const, 3)
            arrived(0, 0)
            for idx in range(NM):
                maxima(0, 0, idx)

            def body(i, q, last):
                if not last:
                    arrived(i + 1, (q + 1) % 4)
                for kt in range(KT):
                    ms = [] if last else [n for n, (st, _, _) in enumerate(RING) if st == kt]
                    tail = [ms.pop()] if kt == KT - 1 and ms else []
                    for n in range(len(SU[kt])):
                        scores(i, q, kt, n)
                        if n % 2 == 0 and ms:
                            maxima(i + 1, (q + 1) % 4, ms.pop(0))
                        if n == min(2, len(SU[kt]) - 1) and kt:
                            weighted(i, q, kt - 1)
                    for idx in ms:
                        maxima(i + 1, (q + 1) % 4, idx)
                    if kt == KT - 1:
                        weighted(i, q, kt)
                    for idx in tail:
                        maxima(i + 1, (q + 1) % 4, idx)

            heads_loop(pe, body)

        @block.scalar
        def _(act):
            act.sem_inc(p_ready, NS)

            def band_exp(i, q, g):
                act.wait_ge(nm_ready, i * NG + g + 1)
                for t in range(g * GROUP, (g + 1) * GROUP):
                    c0, c1 = band_cols(t)
                    last = nc.scalar.activation(band_of(t)[:, c0:c1], band_of(t)[:, c0:c1], ACT.Exp,
                                                bias=nm[:, q % 2, t:t + 1])
                last.then_inc(pb_ready, 1)

            if causal:
                for g in range(NG - 1):
                    band_exp(0, 0, g)

            def body(i, q, last):
                for kt in range(KT):
                    act.wait_ge(pv_done, PVC + i * KT + kt - 3)
                    for n, (j, lo, hi) in enumerate(SU[kt]):
                        u = S_BEFORE[kt] + n
                        act.wait_ge(s_ready, i * NS + u + 1)
                        nc.scalar.activation(pT[:, kt % 4, lo:hi], k.psum[:, 4 + u % 3, 0:hi - lo],
                                             ACT.Exp).then_inc(p_ready, 1)
                    if causal and kt == 1:
                        band_exp(i, q, NG - 1)
                    if causal and not last and kt % GROUP == 1 and kt > 1:
                        band_exp(i + 1, (q + 1) % 4, kt // GROUP - 1)

            heads_loop(act, body)

        @block.vector
        def _(dve):
            dve.sem_inc(pv_done, PVC)
            dve.sem_inc(m_free, MC)
            dve.sem_inc(o_free, 1)
            nc.vector.memset(vh[:, :, :, DH + 1:VP], 0.0)
            nc.vector.memset(vh[:, :, :, DH:DH + 1], 1.0).then_inc(const, 1)
            nc.vector.memset(mx[:, :, :, :], -3e38)
            nc.vector.memset(k_sb[ROW:ROW + 1, :, :], 1.0).then_inc(const, 1)
            nc.vector.tensor_copy(identb, k.ident[:, :]).then_inc(const, 1)
            if causal:
                nc.vector.memset(band_of(0)[:, 0:REL], 0.0).then_inc(const, 1)
            dve.wait_ge(const, 3 + L)

            def maxima(i, q, idx, first=False):
                _, (kind, lo, hi, slot), t = RING[idx]
                r, b = q % 2, 2 * (idx % 2)
                dve.wait_ge(m_ready, i * NM + idx + 1)
                if kind == "far":
                    src = k.psum[:, b:b + 2, :].rearrange("p b n -> p (b n)")[:, 0:hi - lo]
                    nc.vector.reduce_max(mx[:, r, t, slot:slot + 1], src, AX_X).then_inc(m_free, 1)
                elif kind == "band":
                    c0, c1 = band_cols(t)
                    dve.wait_ge(bt_loaded[q], 16 * (i // 4 + 1))
                    if not first:
                        dve.wait_ge(pb_stored[t // GROUP], 16 * GROUP * i)
                    nc.vector.tensor_tensor(band_of(t)[:, c0:c1], k.psum[:, b, c0:c1], bt[:, q, t, c0:c1],
                                            ALU.add).then_inc(band_sum, 1)
                    dve.wait_ge(band_sum, i * KT + t + 1)
                    nc.vector.reduce_max(mx[:, r, t, slot:slot + 1], band_of(t)[:, c0:c1], AX_X).then_inc(m_free, 1)
                else:
                    nc.vector.tensor_copy(q_sb[ROW:ROW + 1, q, lo * BLK:(lo + 1) * BLK],
                                          k.psum[ROW:ROW + 1, b, :]).then_inc(m_free, 1)
                ends = idx + 1 == NM or RING[idx + 1][2] != t or RING[idx + 1][1][0] == "row"
                if kind != "row" and ends and t % GROUP == GROUP - 1:
                    g = t // GROUP
                    ts = slice(g * GROUP, (g + 1) * GROUP)
                    dve.wait_ge(m_free, MC + i * NM + idx + 1)
                    nc.vector.reduce_max(mm[:, r, ts], mx[:, r, ts, :], AX_X).then_inc(mm_ready, 1)
                    dve.wait_ge(mm_ready, i * NG + g + 1)
                    nc.vector.tensor_scalar(nm[:, r, ts], mm[:, r, ts], -1.0, None, ALU.mult).then_inc(nm_ready, 1)

            for idx in range(NM):
                maxima(0, 0, idx, first=True)

            def body(i, q, last):
                if not last:
                    for idx in range(NM):
                        maxima(i + 1, (q + 1) % 4, idx)
                dve.wait_ge(pv_done, PVC + (i + 1) * KT)
                dve.wait_ge(o_stored[q % 2], 16 * (1 + 2 * QB * (i // 2)))
                nc.vector.tensor_copy(osb[:, q % 2, :], k.psum[:, 7, :]).then_inc(o_free, 1)

            heads_loop(dve, body)


def project_stage(k, ctx, causal):
    nc, io = k.nc, k.io
    L = int(causal)
    sem = lambda name: k.semaphore(f"proj{L}_{name}")
    big = k.big
    at = [0]

    def take(n):
        at[0] += n
        return big[:, at[0] - n:at[0]]

    w = take(C * D).rearrange("p (c f) -> p c f", c=C)
    num = take(2 * C * BLK).rearrange("p (r c n) -> p r c n", r=2, c=C)
    rd = take(2 * C * BLK).rearrange("p (r c n) -> p r c n", r=2, c=C)
    o = take(2 * C * BLK).rearrange("p (r c n) -> p r c n", r=2, c=C)
    rec = take(BLK)
    bias = take(D)
    spread = take(P)
    if causal:
        wt = take(2 * H * REL).rearrange("p (r n) -> p r n", r=2)
        wT = take(H * REL // P * BLK).rearrange("p (g n) -> p g n", n=BLK)
        sm = take(C * BLK).rearrange("p (c n) -> p c n", c=C)
        rel = take(DH)
        rel0 = take(DH)
        jmask = take(GROUP)
        dbig = take(GROUP * DH)
    s_w, s_rec, s_rc = sem("weights"), sem("recip_dma"), sem("recip")
    s_ld = [sem(f"loaded{r}") for r in range(2)]
    s_wt = [sem(f"band_loaded{r}") for r in range(2)]
    rb_ready = sem("rb_ready")
    o_ready = sem("o_ready")
    y_ready = sem("y_ready")
    y_free = sem("y_free")
    s_b = sem("bias_added")
    tp_ready = sem("tp_ready")
    tp_free = sem("tp_free")
    ex_ready = sem("ex_ready")
    ex_done = sem("ex_done")
    s_rel = sem("rel")
    W_DMAS = 2 + (GROUP + 2 if causal else 1)
    NGR = H // GROUP

    with nc.Block() as block:
        @block.sync
        def _(sp):
            wv = io[f"attn{L}_w"].rearrange("p (k x) -> p k x", x=C * D)
            sp.dma_start(big[:, 0:C * D], wv[:, 3, :]).then_inc(s_w, 16)
            sp.dma_start(spread[0:HC, :], io["spread"][:, :]).then_inc(s_w, 16)
            if causal:
                for g in range(GROUP):
                    sp.dma_start(rel[g * REL:(g + 1) * REL, :], io["rel"][1:1 + REL, :]).then_inc(s_w, 16)
                sp.dma_start(rel0, io["rel"][0:1, :].to_broadcast([P, DH])).then_inc(s_w, 16)
                sp.dma_start(jmask, io["jmask"][:, :]).then_inc(s_w, 16)
            else:
                sp.dma_start(bias, io["bff"][0:1, :].to_broadcast([P, D])).then_inc(s_w, 16)
            sp.dma_start(rec, k.DD.rearrange("i (b c) -> (i b) c", b=QB)).then_inc(s_rec, 16)
            sp.wait_ge(s_rc, 1)
            sp.dma_start(k.RD.rearrange("i (b c) -> (i b) c", b=QB), rec).then_inc(s_rec, 16)
            sp.wait_ge(s_rec, 32)

            def load(n, half):
                sp.wait_ge(o_ready, (n + 1) * C)
                cols = bass.ds(within(n) * BLK, BLK)
                src = k.ND[bass.ds(batch(n) * D, D), cols]
                sp.dma_start(num[:, half, :, :], src.rearrange("(c p) n -> p c n", p=P)).then_inc(s_ld[half], 16)
                src = k.RD[bass.ds(batch(n) * H, H), cols]
                sp.dma_start(rd[0:HC, half, :, :], src.rearrange("(c h) n -> h c n", h=HC)).then_inc(s_ld[half], 16)
                if causal:
                    for t in range(TB):
                        sp.wait_ge(tp_ready, n * TB + t + 1)
                        tile = bass.DynSlice(batch(n) * H * KT + within(n) * TB + t, H, KT)
                        src = k.PB[tile, 1:1 + P * SKEW].rearrange("h (r c) -> r h c", c=SKEW)[:, :, 0:REL]
                        sp.dma_start(wt[:, t % 2, :].rearrange("p (h j) -> p h j", h=H), src).then_inc(s_wt[t % 2], 16)

            with sp.Fori(0, NBLK // 2) as it:
                for half in range(2):
                    load(it * 2 + half, half)

        @block.tensor
        def _(pe):
            pe.sem_inc(y_ready, 4)
            pe.wait_ge(s_w, 16 * W_DMAS)
            if causal:
                pe.sem_inc(ex_ready, C)
            if causal:
                pe.wait_ge(s_rel, 2)

            def blockwise(n, half, last):
                if causal:
                    for t in range(TB):
                        pe.wait_ge(s_wt[t % 2], 16 * (n * 2 + t // 2 + 1))
                        pe.wait_ge(tp_free, n * TB + t + 1)
                        for g in range(NGR):
                            last_mm = nc.tensor.transpose(k.psum[:, 6 + t % 2, g * P:(g + 1) * P],
                                                          wt[:, t % 2, g * P:(g + 1) * P], k.ident[:, :])
                        last_mm.then_inc(tp_ready, 1)
                    pe.wait_ge(tp_free, 2 + (n + 1) * TB)
                    for c in range(C):
                        pe.wait_ge(o_ready, 2 * C + (n - 1) * C + c + 1)
                        for g2 in range(2):
                            last_mm = nc.tensor.matmul(k.psum[64 * g2:64 * (g2 + 1), 2 + c, :], dbig,
                                                       wT[:, 2 * c + g2, :], start=True, stop=True)
                        last_mm.then_inc(ex_ready, 1)
                pe.wait_ge(s_ld[half], 32 * (n // 2 + 1))
                for c in range(C):
                    pe.wait_ge(o_ready, 2 * C + (n - 1) * C + c + 1)
                    nc.tensor.matmul(k.psum[:, c, :], spread[0:HC, :], rd[0:HC, half, c, :],
                                     start=True, stop=True).then_inc(rb_ready, 1)
                pe.wait_ge(o_ready, 2 * C + (n + 1) * C)
                for pair in range(2):
                    pe.wait_ge(y_free, n * 2 + pair + 1)
                    for t2 in range(2):
                        t = 2 * pair + t2
                        for c in range(C):
                            last_mm = nc.tensor.matmul(k.psum[:, 4 + pair, t2 * D:(t2 + 1) * D],
                                                       o[:, half, c, t * P:(t + 1) * P], w[:, c, :],
                                                       start=(c == 0), stop=(c == C - 1))
                    last_mm.then_inc(y_ready, 1)

            looped(pe, NBLK, blockwise)

        @block.scalar
        def _(act):
            if causal:
                act.sem_inc(tp_free, 2)

                def blockwise(n, half, last):
                    for t in range(TB):
                        act.wait_ge(tp_ready, 2 + n * TB + t + 1)
                        act.wait_ge(ex_ready, C + n * C)
                        nc.scalar.copy(wT[:, :, t * P:(t + 1) * P],
                                       k.psum[:, 6 + t % 2, :].rearrange("p (g n) -> p g n", n=P)).then_inc(tp_free, 1)

                looped(act, NBLK, blockwise)

        @block.vector
        def _(dve):
            dve.sem_inc(o_ready, 2 * C)
            dve.sem_inc(y_free, 2)
            dve.wait_ge(s_rec, 16)
            nc.vector.reciprocal(rec, rec).then_inc(s_rc, 1)
            dve.wait_ge(s_w, 16 * W_DMAS)
            if causal:
                dve.sem_inc(tp_ready, 2)
                nc.vector.tensor_tensor(rel, rel, rel0, ALU.subtract).then_inc(s_rel, 1)
                dve.wait_ge(s_rel, 1)
                nc.vector.tensor_tensor(dbig.rearrange("p (h d) -> p h d", h=GROUP),
                                        rel.unsqueeze(1).to_broadcast([P, GROUP, DH]),
                                        jmask.unsqueeze(2).to_broadcast([P, GROUP, DH]), ALU.mult).then_inc(s_rel, 1)

            def blockwise(n, half, last):
                dve.wait_ge(s_ld[half], 32 * (n // 2 + 1))
                for c in range(C):
                    src = num[:, half, c, :]
                    if causal:
                        dve.wait_ge(ex_ready, C + n * C + c + 1)
                        nc.vector.tensor_tensor(sm[:, c, :], k.psum[:, 2 + c, :], src, ALU.add).then_inc(ex_done, 1)
                        dve.wait_ge(ex_done, n * C + c + 1)
                        src = sm[:, c, :]
                    dve.wait_ge(rb_ready, n * C + c + 1)
                    if c == 0:
                        dve.wait_ge(y_ready, 4 + (n - 1) * 2)
                    nc.vector.tensor_tensor(o[:, half, c, :], k.psum[:, c, :], src, ALU.mult).then_inc(o_ready, 1)
                for pair in range(2):
                    tiles = k.X[:, bass.ds(n * TB + 2 * pair, 2), :]
                    if not causal:
                        nc.vector.tensor_tensor(tiles, tiles, bias.unsqueeze(1).to_broadcast([P, 2, D]),
                                                ALU.add).then_inc(s_b, 1)
                        dve.wait_ge(s_b, n * 2 + pair + 1)
                    dve.wait_ge(y_ready, 4 + n * 2 + pair + 1)
                    nc.vector.tensor_tensor(tiles, k.psum[:, 4 + pair, :].rearrange("p (t n) -> p t n", t=2), tiles,
                                            ALU.add).then_inc(y_free, 1)

            looped(dve, NBLK, blockwise)


def lstm_stage(k, ctx, run):
    nc, io = k.nc, k.io
    sem = lambda name: k.semaphore(f"lstm{run}_{name}")
    big = k.big
    at = [0]

    def take(n):
        at[0] += n
        return big[:, at[0] - n:at[0]]

    w = k.arena[:, 0:8 * C * D].rearrange("p (k c f) -> p k c f", k=8, c=C)
    xT = take(2 * 2 * C * BLK).rearrange("p (r t c n) -> p r t c n", r=2, t=2, c=C)
    gates = take(2 * 3 * C * BLK).rearrange("p (s g c n) -> p s g c n", s=2, g=3, c=C)
    ig = take(C * BLK).rearrange("p (c n) -> p c n", c=C)
    cell = take(2 * C * BLK).rearrange("p (s c n) -> p s c n", s=2, c=C)
    fc = take(C * BLK).rearrange("p (c n) -> p c n", c=C)
    pre = take(2 * BLK).rearrange("p (r n) -> p r n", r=2)
    th = take(2 * BLK).rearrange("p (r n) -> p r n", r=2)
    b = take(4 * C).rearrange("p (k c) -> p k c", k=4)
    b0 = take(3 * C).rearrange("p (k c) -> p k c", k=3)
    bo = take(D)
    NBK = S // BLK
    NU = 3 * C
    NO = 2 * TB // 2
    NT = 2 * C

    ln = LayerNorm(k, sem)
    s_w, s_b0 = sem("weights"), sem("b0")
    t_ready, t_free = sem("t_ready"), sem("t_free")
    g_ready = sem("g_ready")
    g_done = sem("g_done")
    ig_done = sem("ig_done")
    c_ready = sem("c_ready")
    o_ready = sem("o_ready")
    pre_done = sem("pre_done")
    th_done = sem("th_done")
    x_done = sem("x_done")

    with nc.Block() as block:
        @block.sync
        def _(sp):
            sp.dma_start(k.arena[:, 0:8 * C * D], io["lstm_w"][:, :]).then_inc(s_w, 16)
            sp.dma_start(b, io["lstm_b"][:, :, :]).then_inc(s_w, 16)
            sp.dma_start(bo, io["bo"][0:1, :].to_broadcast([P, D])).then_inc(s_w, 16)

        @block.gpsimd
        def _(pool):
            def both(m):
                for t in range(2):
                    ln.pool_rstd(pool, m + t, t)

            both(0)
            with pool.Fori(1, NBK) as n:
                both(n * 2)

        @block.tensor
        def _(pe):
            def transposes(n, first=False):
                for i in range(NT):
                    t, c = i // C, i % C
                    if c == 0:
                        pe.wait_ge(ln.xn, n * 2 + t + 1)
                    if i == 0 and not first:
                        pe.wait_ge(pre_done, (n - 1) * NO + 2)
                    pe.wait_ge(t_free, n * NT + i + 1)
                    ln.pe_transpose(t, c, 6 + c).then_inc(t_ready, 1)

            pe.wait_ge(s_w, 16 * 3)
            for g in range(3):
                for m in range(C):
                    for c in range(C):
                        last_mm = nc.tensor.matmul(k.psum[:, 5, g * C + m:g * C + m + 1],
                                                   w[:, 2 * g + 1, c, m * P:(m + 1) * P], b[:, 3, c:c + 1],
                                                   start=(c == 0), stop=(c == C - 1))
            last_mm.then_inc(s_b0, 1)
            pe.wait_ge(s_b0, 2)
            transposes(0, first=True)

            def blockwise(n, r, last):
                pe.wait_ge(t_free, 2 + (n + 1) * NT)
                for u in range(NU):
                    g, m = u // C, u % C
                    pe.wait_ge(g_done, n * 2 * NU + u + 1)
                    for c in range(C):
                        last_mm = nc.tensor.matmul(k.psum[:, u, :], w[:, 2 * g, c, m * P:(m + 1) * P],
                                                   xT[:, r, 0, c, :], start=(c == 0), stop=(c == C - 1))
                    last_mm.then_inc(g_ready, 1)
                for u in range(NU):
                    g, m = u // C, u % C
                    pe.wait_ge(g_done, n * 2 * NU + NU + u + 1)
                    for c in range(C):
                        nc.tensor.matmul(k.psum[:, u, :], w[:, 2 * g, c, m * P:(m + 1) * P],
                                         xT[:, r, 1, c, :], start=(c == 0), stop=False)
                pe.wait_ge(c_ready, n * 2 * C + C)
                for u in range(NU):
                    g, m = u // C, u % C
                    for c in range(C):
                        last_mm = nc.tensor.matmul(k.psum[:, u, :], w[:, 2 * g + 1, c, m * P:(m + 1) * P],
                                                   cell[:, 0, c, :], start=False, stop=(c == C - 1))
                    last_mm.then_inc(g_ready, 1)
                if not last:
                    transposes(n + 1)
                pe.wait_ge(c_ready, n * 2 * C + 2 * C)
                for i in range(NO):
                    t, pair = i // 2, i % 2
                    if not last:
                        pe.wait_ge(t_free, 2 + (n + 2) * NT)
                    pe.wait_ge(pre_done, n * NO + i + 1)
                    for t2 in range(2):
                        tile = slice((2 * pair + t2) * P, (2 * pair + t2 + 1) * P)
                        out = k.psum[:, 6 + pair, t2 * D:(t2 + 1) * D]
                        for c in range(C):
                            nc.tensor.matmul(out, xT[:, r, t, c, tile], w[:, 6, c, :], start=(c == 0), stop=False)
                        for c in range(C):
                            last_mm = nc.tensor.matmul(out, cell[:, 1, c, tile], w[:, 7, c, :],
                                                       start=False, stop=(c == C - 1))
                    last_mm.then_inc(o_ready, 1)

            looped(pe, NBK, blockwise)

        @block.scalar
        def _(act):
            act.sem_inc(t_free, 2)
            act.sem_inc(g_done, NU)

            def chunks(n, r):
                for i in range(NT):
                    act.wait_ge(t_ready, n * NT + i + 1)
                    nc.scalar.copy(xT[:, r, i // C, i % C, :], k.psum[:, 6 + i % C, :]).then_inc(t_free, 1)

            chunks(0, 0)
            act.wait_ge(s_b0, 2)

            def blockwise(n, r, last):
                for s in range(2):
                    bias = b if s else b0
                    for u in range(NU):
                        g, m = u // C, u % C
                        act.wait_ge(g_ready, n * 2 * NU + s * NU + u + 1)
                        nc.scalar.activation(gates[:, s, g, m, :], k.psum[:, u, :],
                                             ACT.Tanh if g == 2 else ACT.Sigmoid,
                                             bias=bias[:, g, m:m + 1]).then_inc(g_done, 1)
                if not last:
                    chunks(n + 1, 1 - r)
                for i in range(NO):
                    act.wait_ge(pre_done, 2 + n * NO + i + 1)
                    act.wait_ge(x_done, n * NO + i + 1)
                    nc.scalar.activation(th[:, i % 2, :], pre[:, i % 2, :], ACT.Tanh).then_inc(th_done, 1)

            looped(act, NBK, blockwise)

        @block.vector
        def _(dve):
            dve.sem_inc(pre_done, 2)
            dve.sem_inc(x_done, 2)
            dve.wait_ge(s_w, 16 * 3)

            def normalize(n):
                for t in range(2):
                    ln.dve_stats(dve, n * 2 + t, t, n * TB + t * (TT // NB))
                for t in range(2):
                    ln.dve_apply(dve, n * 2 + t, t, n * TB + t * (TT // NB))

            normalize(0)
            dve.wait_ge(s_b0, 1)
            nc.vector.tensor_tensor(b0, k.psum[:, 5, 0:NU].rearrange("p (g c) -> p g c", g=3), b[:, 0:3, :],
                                    ALU.add).then_inc(s_b0, 1)

            def state(n, s):
                base = n * 3 * C + (C if s else 0)
                for m in range(C):
                    dve.wait_ge(g_done, NU + n * 2 * NU + s * NU + 2 * C + m + 1)
                    nc.vector.tensor_tensor(ig[:, m, :], gates[:, s, 1, m, :], gates[:, s, 2, m, :],
                                            ALU.mult).then_inc(ig_done, 1)
                    if s:
                        nc.vector.tensor_tensor(fc[:, m, :], gates[:, s, 0, m, :], cell[:, 0, m, :],
                                                ALU.mult).then_inc(ig_done, 1)
                        dve.wait_ge(ig_done, base + 2 * m + 2)
                        nc.vector.tensor_tensor(cell[:, 1, m, :], fc[:, m, :], ig[:, m, :], ALU.add).then_inc(c_ready, 1)
                    else:
                        dve.wait_ge(ig_done, base + m + 1)
                        nc.vector.scalar_tensor_tensor(cell[:, 0, m, :], gates[:, s, 0, m, :], b[:, 3, m:m + 1],
                                                       ig[:, m, :], ALU.mult, ALU.add).then_inc(c_ready, 1)

            def update(n, i):
                t, pair = i // 2, i % 2
                dve.wait_ge(th_done, n * NO + i + 1)
                tiles = k.X[:, bass.ds(n * TB + t * (TT // NB) + 2 * pair, 2), :]
                nc.vector.scalar_tensor_tensor(tiles, th[:, i % 2, :].rearrange("p (t n) -> p t n", t=2), 0.5, tiles,
                                               ALU.mult, ALU.add).then_inc(x_done, 1)

            def blockwise(n, r, last):
                state(n, 0)
                if not last:
                    normalize(n + 1)
                dve.wait_ge(c_ready, n * 2 * C + C)
                state(n, 1)
                for i in range(NO):
                    dve.wait_ge(o_ready, n * NO + i + 1)
                    nc.vector.tensor_tensor(pre[:, i % 2, :].rearrange("p (t n) -> p t n", t=2),
                                            k.psum[:, 6 + i % 2, :].rearrange("p (t n) -> p t n", t=2),
                                            bo.unsqueeze(1).to_broadcast([P, 2, D]), ALU.add).then_inc(pre_done, 1)
                    if i:
                        update(n, i - 1)
                update(n, NO - 1)

            looped(dve, NBK, blockwise)




def store_stage(k, ctx):
    nc, io = k.nc, k.io
    s_out = k.semaphore("s_out")
    with nc.Block() as block:
        @block.sync
        def _(sp):
            o_t = io["out"].rearrange("b (t p) d -> p (b t) d", p=P)
            for i in range(4):
                n = TT // 4
                sp.dma_start(o_t[:, i * n:(i + 1) * n, :], k.X[:, i * n:(i + 1) * n, :]).then_inc(s_out, 16)
            sp.wait_ge(s_out, 16 * 4)


def program(nc, io, stages):
    with ExitStack() as ctx:
        k = alloc(nc, ctx, io)
        alloc_attention(k, ctx)
        load_stage(k, ctx)
        k.free_semaphores()
        for st in stages:
            st(k, ctx)
            k.free_semaphores()
        store_stage(k, ctx)


def attention(causal):
    def stage(k, ctx):
        qkv_stage(k, ctx, causal)
        k.free_semaphores()
        heads_stage(k, ctx, causal)
        k.free_semaphores()
        project_stage(k, ctx, causal)
    return stage


STAGES = [lambda k, ctx: moe_stage(k, ctx, 0), attention(False), lambda k, ctx: moe_stage(k, ctx, 1),
          lambda k, ctx: lstm_stage(k, ctx, 0), attention(True), lambda k, ctx: lstm_stage(k, ctx, 1)]


def _tables():
    f = np.float32
    inv = (f(1.0) / f(10000.0) ** (np.arange(0, DH, 2, dtype=f) / f(DH))).astype(f)
    ang = np.outer(np.arange(S, dtype=f), inv).astype(f)
    cos, sin = np.cos(ang).astype(f), np.sin(ang).astype(f)
    pair = (np.arange(P) % DH) // 2
    sign = np.where(np.arange(P) % 2 == 0, f(-1), f(1))[:, None]
    rope = np.stack([cos.T[pair], sign * sin.T[pair]], axis=1).astype(f)
    r, c = np.arange(P)[:, None], np.arange(SKEW)[None, :]
    mask = np.where(c - REL > r, f(NEG), f(0)).astype(f)
    hm = (np.arange(P)[:, None] // DH == np.arange(HC)[None, :]).astype(f)
    spread = np.ascontiguousarray(hm.T)
    jm = (np.arange(P)[:, None] // REL == np.arange(GROUP)[None, :]).astype(f)
    return {"rope": rope, "bias0": mask, "hmask": hm, "jmask": jm, "spread": spread}


def _feature_major(ws):
    w = np.stack([np.asarray(x).T for x in ws])
    n, i, o = w.shape
    return np.ascontiguousarray(w.reshape(n, C, P, o).transpose(2, 0, 1, 3).reshape(P, n * C * o))


def kernel(**inputs):
    import numpy as _np
    import concourse.bacc as _bacc
    from concourse import mybir as _mybir
    from concourse.bass_utils import run_bass_kernel_spmd as _run

    a = {n: _np.asarray(v) for n, v in inputs.items()}
    arrays = {"x": a["L0_attn_x"]}
    moe = []
    for e in range(E):
        moe += [a["L0_ffn_ew1"][e], a["L0_ffn_ew3"][e], a["L0_ffn_ew2"][e]]
    moe += [a["L0_ffn_fc1"], a["L0_ffn_fc2"], a["L0_ffn_fc3"]]
    arrays["moe_w"] = _feature_major(moe)
    arrays["gwT"] = _np.ascontiguousarray(a["L0_ffn_gate_w"].T.reshape(C, P, E).transpose(1, 0, 2))
    arrays["gb"] = a["L0_ffn_gate_b"].reshape(E, 1)
    arrays["attn0_w"] = _feature_major([a["L0_attn_Wq"], a["L0_attn_Wk"], a["L0_attn_Wv"], a["L0_attn_Wff"]])
    arrays["bff"] = a["L0_attn_bff"].reshape(1, D)
    swap = _np.arange(D).reshape(D // 2, 2)[:, ::-1].reshape(D)
    arrays["attn1_w"] = _feature_major([a["L1_attn_w_q"], a["L1_attn_w_k"], a["L1_attn_w_v"], a["L1_attn_w_o"],
                                        a["L1_attn_w_q"][swap], a["L1_attn_w_k"][swap]])
    arrays["rel"] = a["L1_attn_rel_emb"]
    arrays["relT"] = _np.tile(a["L1_attn_rel_emb"][:1 + REL].T, (HC, 1))
    arrays["lstm_w"] = _feature_major([a["L1_ffn_" + n] for n in ("wf", "uf", "wi", "ui", "wc", "uc", "wo", "uo")])
    arrays["lstm_b"] = _np.ascontiguousarray(
        _np.stack([a["L1_ffn_" + n] for n in ("bf", "bi", "bc", "in_c")]).reshape(4, C, P).transpose(2, 0, 1))
    arrays["bo"] = a["L1_ffn_bo"].reshape(1, D)
    arrays.update(_tables())
    arrays["ident"] = _np.eye(P, dtype=_np.float32)
    arrays["tie"] = _np.tile(_np.tril(_np.ones((E, E), _np.float32), -1).reshape(1, E * E), (P, 1))

    nc = _bacc.Bacc("TRN2", target_bir_lowering=False, num_devices=1)
    maps, io = {}, {}
    for name, v in arrays.items():
        v = _np.ascontiguousarray(v)
        maps[f"in_{name}"] = v
        io[name] = nc.dram_tensor(f"in_{name}", v.shape, _mybir.dt.from_np(v.dtype), kind="ExternalInput").ap()
    io["out"] = nc.dram_tensor("out_0", (NB, S, D), _mybir.dt.float32, kind="ExternalOutput").ap()
    program(nc, io, STAGES)
    r = _run(nc, [maps], core_ids=[0])
    return r.results[0]["out_0"]
```

```python
from contextlib import ExitStack

import numpy as np

import concourse.bass as bass
from concourse import mybir

ALU = mybir.AluOpType
ACT = mybir.ActivationFunctionType
F32 = mybir.dt.float32
BF16 = mybir.dt.bfloat16
F32R = mybir.dt.float32r
AX_X = mybir.AxisListType.X

P = 128
D = 256
C = D // P
NB, S = 2, 2048
TOK = NB * S
TT = TOK // P
BLK = 512
TB = BLK // P
NBLK = TOK // BLK
TOP_K = 2
E = 6
H, DH = 16, 16
HC = P // DH
EPS = 1e-5


class Core:

    def __init__(self, nc, io):
        self.nc, self.io = nc, io
        self.taken = []
        self.scratch = 0

    def semaphore(self, name):
        s = self.nc.alloc_semaphore(name=name)
        self.taken.append(s)
        return s

    def free_semaphores(self):
        nums = sorted(s.num for s in self.taken)
        first = [n for n in nums if n - 1 not in nums]
        after = [n + 1 for n in nums if n + 1 not in nums]
        with self.nc.Block() as block:
            @block.sync
            def _(sp):
                for lo, hi in zip(first, after):
                    sp.sem_clear(range(lo, hi))
        for s in self.taken:
            self.nc.release_semaphore(s)
        self.taken = []


def alloc(nc, ctx, io):
    k = Core(nc, io)

    def sb(name, shape, dt=F32):
        return ctx.enter_context(nc.sbuf_tensor(name, shape, dt))

    k.X = sb("X", [P, TT, D])
    k.xn = sb("xn", [P, 2, TB, D])
    k.st = sb("st", [P, 2, TB, 6])
    k.lnv = sb("lnv", [P, 2, 6, TB])
    k.ident = sb("ident_sb", [P, P])
    k.neghalf = sb("neghalf", [P, TB])
    k.psum = ctx.enter_context(nc.psum_tensor("psum", [P, 8, BLK], F32))
    return k


def alloc_scratch(k, ctx):
    n = k.scratch = k.scratch + 1

    def sb(name, shape):
        return ctx.enter_context(k.nc.sbuf_tensor(f"{name}{n}", shape, F32))

    k.xT = sb("xT", [P, 2, C, BLK])
    k.arena = sb("arena", [P, 21 * C * D])
    k.big = sb("big", [P, 19 * 1024])
    k.V = sb("values", [P, NB, H, KT, DH])


class LayerNorm:

    def __init__(self, k, sem):
        self.k = k
        self.dve = sem("ln_dve")
        self.var = sem("ln_var")
        self.rstd = sem("ln_rstd")
        self.xn = sem("ln_xn")
        self.DVE_STEPS = 3

    def dve_stats(self, dve, n, half, g):
        k, nc = self.k, self.k.nc
        base = n * self.DVE_STEPS
        st, v = k.st[:, half, :, :], k.lnv
        for t in range(TB):
            last = nc.vector.bn_stats(st[:, t, :], k.X[:, bass.ds(g + t, 1), :])
        last.then_inc(self.dve, 1)
        dve.wait_ge(self.dve, base + 1)
        nc.vector.tensor_tensor(v[:, half, 0, :], st[:, :, 1], st[:, :, 4], ALU.add)
        nc.vector.tensor_tensor(v[:, half, 1, :], st[:, :, 1], st[:, :, 4], ALU.subtract)
        nc.vector.tensor_tensor(v[:, half, 2, :], st[:, :, 2], st[:, :, 5], ALU.add).then_inc(self.dve, 1)
        dve.wait_ge(self.dve, base + 2)
        nc.vector.tensor_scalar(v[:, half, 0, :], v[:, half, 0, :], 0.5, None, ALU.mult)
        nc.vector.scalar_tensor_tensor(v[:, half, 3, :], v[:, half, 1, :], 0.25, v[:, half, 1, :],
                                       ALU.mult, ALU.mult)
        nc.vector.tensor_scalar(v[:, half, 2, :], v[:, half, 2, :], 1.0 / D, EPS,
                                ALU.mult, ALU.add).then_inc(self.dve, 1)
        dve.wait_ge(self.dve, base + 3)
        nc.vector.tensor_tensor(v[:, half, 4, :], v[:, half, 2, :], v[:, half, 3, :],
                                ALU.add).then_inc(self.var, 1)

    def pool_rstd(self, pool, n, half):
        k, nc = self.k, self.k.nc
        pool.wait_ge(self.var, n + 1)
        nc.gpsimd.tensor_tensor(k.lnv[:, half, 5, :], k.lnv[:, half, 4, :], k.neghalf[:, :],
                                ALU.pow).then_inc(self.rstd, 1)

    def dve_apply(self, dve, n, half, g):
        k, nc = self.k, self.k.nc
        dve.wait_ge(self.rstd, n + 1)
        for t in range(TB):
            last = nc.vector.tensor_scalar(k.xn[:, half, t, :], k.X[:, bass.ds(g + t, 1), :].rearrange("p a d -> p (a d)"),
                                           k.lnv[:, half, 0, t:t + 1], k.lnv[:, half, 5, t:t + 1],
                                           ALU.subtract, ALU.mult)
        last.then_inc(self.xn, 1)

    def pe_transpose(self, half, c, bank):
        k, nc = self.k, self.k.nc
        for t in range(TB):
            last = nc.tensor.transpose(k.psum[:, bank, t * P:(t + 1) * P],
                                       k.xn[:, half, t, c * P:(c + 1) * P], k.ident[:, :])
        return last


def looped(eng, blocks, body):
    with eng.Fori(0, blocks // 2 - 1) as it:
        for half in range(2):
            body(it * 2 + half, half, False)
    for half in range(2):
        body(blocks - 2 + half, half, half == 1)


def looped_after_first(eng, blocks, first, body):
    first()
    body(1, 1, False)
    with eng.Fori(1, blocks // 2 - 1) as it:
        for half in range(2):
            body(it * 2 + half, half, False)
    for half in range(2):
        body(blocks - 2 + half, half, half == 1)


def load_stage(k, ctx):
    nc, io = k.nc, k.io
    s_in = k.semaphore("s_in")
    with nc.Block() as block:
        @block.sync
        def _(sp):
            x_t = io["x"].rearrange("b (t p) d -> p (b t) d", p=P)
            for i in range(4):
                n = TT // 4
                sp.dma_start(k.X[:, i * n:(i + 1) * n, :], x_t[:, i * n:(i + 1) * n, :]).then_inc(s_in, 16)
            sp.dma_start(k.ident[:, :], io["ident"][:, :]).then_inc(s_in, 16)
            sp.wait_ge(s_in, 16 * 5)

        @block.vector
        def _(dve):
            nc.vector.memset(k.neghalf[:, :], -0.5)


def moe_stage(k, ctx, run):
    nc, io = k.nc, k.io
    sem = lambda name: k.semaphore(f"moe{run}_{name}")
    with ExitStack() as local:
        def sb(name, shape, dt=F32):
            return local.enter_context(nc.sbuf_tensor(f"moe{run}_{name}", shape, dt))

        NW = 3 * C * D
        w_in = sb("w_in", [P, 2, NW])
        w_parts = [sb(f"w_{x}", [P, (E + 1) * NW], F32R) for x in ("hi", "lo")]
        W = [v[:, :].rearrange("p (e k c f) -> p e k c f", e=E + 1, k=3, c=C) for v in w_parts]
        xhi = sb("x_hi", [P, 2, C, BLK], F32R)
        xlo = sb("x_lo", [P, 2, C, BLK], F32R)
        h = sb("h_hi", [P, 2, C, BLK], F32R)
        h_lo = sb("h_lo", [P, 2, C, BLK], F32R)
        hf = sb("h", [P, 2, BLK])
        sg = sb("sg", [P, 2, BLK])
        ts = sb("ts", [P, 2, BLK])
        PARTS = ((0, 0), (0, 1), (1, 0))
        gwT = sb("gwT", [P, C, E])
        gb = sb("gb", [E, 1])
        pT = sb("pT", [P, 2, BLK])
        pr = sb("pr", [P, 2, TB, E])
        gt = sb("gt", [P, 2, TB, E, E])
        eq = sb("eq", [P, 2, TB, E, E])
        tie = sb("tie", [P, E * E])
        rank = sb("rank", [P, 2, TB, E])
        wsel = sb("wsel", [P, 2, TB, E])
        tot = sb("tot", [P, 2, TB])
        ge = sb("ge", [P, 2, TB, E])

        ln = LayerNorm(k, sem)
        s_w = sem("weights")
        s_zero = sem("zero")
        t_ready = sem("t_ready")
        t_free = sem("t_free")
        up_ready = sem("up_ready")
        sg_ready = sem("sg_ready")
        ts_ready = sem("ts_ready")
        h_ready = sem("h_ready")
        dn_ready = sem("dn_ready")
        x_upd = sem("x_upd")
        g_dve = sem("g_dve")
        g_tot = sem("g_tot")
        ge_ready = sem("ge_ready")
        s_in = [sem(f"w_in{r}") for r in range(2)]
        w_hi, w_lo = sem("w_hi"), sem("w_lo")
        xl_ready = sem("xl_ready")
        hh_ready = sem("hh_ready")
        hl_ready = sem("hl_ready")
        U = C * (E + 1)
        CREDIT = 2

        with nc.Block() as block:
            @block.sync
            def _(sp):
                sp.wait_ge(s_zero, 1)
                sp.dma_start(gwT[:, :, :], io["gwT"][:, :, :]).then_inc(s_w, 16)
                sp.dma_start(gb[:, :], io["gb"][:, :]).then_inc(s_w, 16)
                sp.dma_start(tie[:, :], io["tie"][:, :]).then_inc(s_w, 16)
                for e in range(E + 1):
                    if e >= 2:
                        sp.wait_ge(w_lo, e - 1)
                    sp.dma_start(w_in[:, e % 2, :], io["moe_w"][:, e * NW:(e + 1) * NW]).then_inc(s_in[e % 2], 16)

            @block.gpsimd
            def _(pool):
                nc.gpsimd.memset(pT[:, :, :], 0.0).then_inc(s_zero, 1)
                ln.pool_rstd(pool, 0, 0)

                def blockwise(n, half, last):
                    for u in range(U):
                        if u == 2 and not last:
                            ln.pool_rstd(pool, n + 1, 1 - half)
                        pool.wait_ge(hh_ready, n * U + u + 1)
                        r = (half + u // C) % 2
                        nc.gpsimd.tensor_tensor(h_lo[:, r, u % C, :], hf[:, u % 2, :],
                                                h[:, r, u % C, :].bitcast(F32), ALU.subtract).then_inc(hl_ready, 1)

                looped(pool, NBLK, blockwise)

            @block.tensor
            def _(pe):
                def transpose(n, half, c):
                    if c == 0:
                        pe.wait_ge(ln.xn, n + 1)
                    pe.wait_ge(t_free, n * 4 + c + 1)
                    ln.pe_transpose(half, c, 6 + c).then_inc(t_ready, 1)

                def gate(n, half):
                    pe.wait_ge(t_free, n * 4 + 2 + CREDIT)
                    pe.wait_ge(xl_ready, (n + 1) * C)
                    for x, part in enumerate((xhi, xlo)):
                        for c in range(C):
                            last = nc.tensor.matmul(k.psum[0:E, 6, :], gwT[:, c, :], part[:, half, c, :].bitcast(F32),
                                                    start=(x == 0 and c == 0), stop=(x == 1 and c == C - 1))
                    last.then_inc(t_ready, 1)

                def gate_transpose(n, half):
                    pe.wait_ge(t_free, n * 4 + 3 + CREDIT)
                    for t in range(TB):
                        last = nc.tensor.transpose(k.psum[:, 7, t * P:(t + 1) * P],
                                                   pT[:, half, t * P:(t + 1) * P], k.ident[:, :])
                    last.then_inc(t_ready, 1)

                def up(n, half, e):
                    pe.wait_ge(w_lo, e + 1)
                    for m in range(C):
                        u = 2 * e + m
                        pe.wait_ge(h_ready, n * U + u + 1)
                        for kind in range(2):
                            for c in range(C):
                                for wp, xp in PARTS:
                                    last = nc.tensor.matmul(k.psum[:, 2 * (u % 2) + kind, :],
                                                            W[wp][:, e, kind, c, m * P:(m + 1) * P],
                                                            (xhi, xlo)[xp][:, half, c, :],
                                                            start=(c == 0 and wp + xp == 0), stop=(c == C - 1 and wp == 1))
                        last.then_inc(up_ready, 1)

                def down(n, half, e):
                    pe.wait_ge(hl_ready, n * U + 2 * e + 2 + CREDIT)
                    for pair in range(2):
                        pe.wait_ge(x_upd, n * U + 2 * e + pair + 1)
                        for t2 in range(2):
                            t = 2 * pair + t2
                            for c in range(C):
                                for wp, xp in PARTS:
                                    last = nc.tensor.matmul(k.psum[:, 4 + pair, t2 * D:(t2 + 1) * D],
                                                            (h, h_lo)[xp][:, (half + e) % 2, c, t * P:(t + 1) * P],
                                                            W[wp][:, e, 2, c, :],
                                                            start=(c == 0 and wp + xp == 0), stop=(c == C - 1 and wp == 1))
                        last.then_inc(dn_ready, 1)

                pe.wait_ge(s_w, 16 * 3)
                transpose(0, 0, 0)
                transpose(0, 0, 1)
                gate(0, 0)
                gate_transpose(0, 0)

                up(0, 0, 0)

                def blockwise(n, half, last):
                    for e in range(E + 1):
                        if e < E:
                            up(n, half, e + 1)
                        if not last:
                            if e == 3:
                                transpose(n + 1, 1 - half, 0)
                                transpose(n + 1, 1 - half, 1)
                            if e == 5:
                                gate(n + 1, 1 - half)
                            if e == 6:
                                gate_transpose(n + 1, 1 - half)
                                up(n + 1, 1 - half, 0)
                        down(n, half, e)

                looped(pe, NBLK, blockwise)

            @block.scalar
            def _(act):
                act.sem_inc(t_free, CREDIT)

                def misc(n, half, i):
                    act.wait_ge(t_ready, n * 4 + i + 1)
                    if i < 2:
                        ins = nc.scalar.copy(xhi[:, half, i, :], k.psum[:, 6 + i, :])
                    elif i == 2:
                        ins = nc.scalar.activation(pT[0:E, half, :], k.psum[0:E, 6, :], ACT.Sigmoid, bias=gb[:, 0:1])
                    else:
                        ins = nc.scalar.copy(pr[:, half, :, :], k.psum[:, 7, :].rearrange("p (t n) -> p t n", t=TB)[:, :, 0:E])
                    ins.then_inc(t_free, 1)

                act.wait_ge(s_w, 16 * 3)
                misc(0, 0, 0)
                misc(0, 0, 1)

                def split(e):
                    act.wait_ge(s_in[e % 2], 16 * (e // 2 + 1))
                    nc.scalar.copy(w_parts[0][:, e * NW:(e + 1) * NW], w_in[:, e % 2, :]).then_inc(w_hi, 1)

                split(0)
                misc(0, 0, 2)
                misc(0, 0, 3)
                split(1)

                def upper(n, half, u):
                    act.wait_ge(h_ready, n * U + u + 1 + CREDIT)
                    nc.scalar.copy(h[:, (half + u // C) % 2, u % C, :], hf[:, u % 2, :]).then_inc(hh_ready, 1)

                def blockwise(n, half, last, first=False):
                    for u in range(U):
                        if first and u % C == 0 and u // C + 2 <= E:
                            split(u // C + 2)
                        act.wait_ge(up_ready, n * U + u + 1)
                        act.wait_ge(ts_ready, n * U + u + 1)
                        nc.scalar.activation(sg[:, u % 2, :], k.psum[:, 2 * (u % 2), :],
                                             ACT.Sigmoid).then_inc(sg_ready, 1)
                        upper(n, half, u)
                        if not last and u in (9, 10):
                            misc(n + 1, 1 - half, u - 9)
                    if not last:
                        misc(n + 1, 1 - half, 2)
                        misc(n + 1, 1 - half, 3)

                looped_after_first(act, NBLK, lambda: blockwise(0, 0, False, True), blockwise)

            @block.vector
            def _(dve):
                dve.sem_inc(ts_ready, CREDIT)
                dve.sem_inc(h_ready, CREDIT)
                dve.sem_inc(hl_ready, CREDIT)
                dve.sem_inc(x_upd, CREDIT)

                def gate(n, half):
                    base = n * 6
                    p = pr[:, half, :, :]
                    mine = p.unsqueeze(3).to_broadcast([P, TB, E, E])
                    other = p.unsqueeze(2).to_broadcast([P, TB, E, E])
                    dve.wait_ge(t_free, n * 4 + 4 + CREDIT)
                    nc.vector.tensor_tensor(gt[:, half], other, mine, ALU.is_gt)
                    nc.vector.tensor_tensor(eq[:, half], other, mine, ALU.is_equal).then_inc(g_dve, 1)
                    dve.wait_ge(g_dve, base + 1)
                    tie_b = tie[:, :].rearrange("p (e i) -> p e i", e=E).unsqueeze(1).to_broadcast([P, TB, E, E])
                    nc.vector.tensor_tensor(eq[:, half], eq[:, half], tie_b, ALU.mult).then_inc(g_dve, 1)
                    dve.wait_ge(g_dve, base + 2)
                    nc.vector.tensor_tensor(gt[:, half], gt[:, half], eq[:, half], ALU.add).then_inc(g_dve, 1)
                    dve.wait_ge(g_dve, base + 3)
                    nc.vector.reduce_sum(rank[:, half], gt[:, half], AX_X).then_inc(g_dve, 1)
                    dve.wait_ge(g_dve, base + 4)
                    nc.vector.scalar_tensor_tensor(wsel[:, half], rank[:, half], TOP_K - 0.5, p,
                                                   ALU.is_lt, ALU.mult).then_inc(g_dve, 1)
                    dve.wait_ge(g_dve, base + 5)
                    nc.vector.reduce_sum(tot[:, half], wsel[:, half], AX_X).then_inc(g_dve, 1)
                    dve.wait_ge(g_dve, base + 6)
                    nc.vector.tensor_scalar(tot[:, half], tot[:, half], 1e-8, None, ALU.add).then_inc(g_tot, 1)
                    dve.wait_ge(g_tot, n * 2 + 1)
                    nc.vector.reciprocal(tot[:, half], tot[:, half]).then_inc(g_tot, 1)
                    dve.wait_ge(g_tot, n * 2 + 2)
                    nc.vector.scalar_tensor_tensor(ge[:, half], wsel[:, half], 0.5,
                                                   tot[:, half].unsqueeze(2).to_broadcast([P, TB, E]),
                                                   ALU.mult, ALU.mult).then_inc(ge_ready, 1)

                def hidden(n, e):
                    for m in range(C):
                        u = 2 * e + m
                        dve.wait_ge(sg_ready, n * U + u + 1)
                        nc.vector.tensor_tensor(ts[:, u % 2, :], k.psum[:, 2 * (u % 2), :], sg[:, u % 2, :],
                                                ALU.mult).then_inc(ts_ready, 1)
                        dve.wait_ge(ts_ready, n * U + u + 1 + CREDIT)
                        dve.wait_ge(hl_ready, n * U + u + 1)
                        nc.vector.tensor_tensor(hf[:, u % 2, :], k.psum[:, 2 * (u % 2) + 1, :], ts[:, u % 2, :],
                                                ALU.mult).then_inc(h_ready, 1)

                def update(n, half, e):
                    for pair in range(2):
                        d = 2 * e + pair
                        dve.wait_ge(dn_ready, n * U + d + 1)
                        dve.wait_ge(x_upd, n * U + d - 1 + CREDIT)
                        for t2 in range(2):
                            t = 2 * pair + t2
                            xt = k.X[:, bass.ds(n * TB + t, 1), :].rearrange("p a d -> p (a d)")
                            w = ge[:, half, t, e:e + 1] if e < E else 0.5
                            last = nc.vector.scalar_tensor_tensor(xt, k.psum[:, 4 + pair, t2 * D:(t2 + 1) * D], w, xt,
                                                                  ALU.mult, ALU.add)
                        last.then_inc(x_upd, 1)

                def lower(n, half):
                    for c in range(C):
                        dve.wait_ge(t_free, n * 4 + c + 1 + CREDIT)
                        nc.vector.tensor_tensor(xlo[:, half, c, :], k.psum[:, 6 + c, :],
                                                xhi[:, half, c, :].bitcast(F32), ALU.subtract).then_inc(xl_ready, 1)

                ln.dve_stats(dve, 0, 0, 0)
                ln.dve_apply(dve, 0, 0, 0)
                lower(0, 0)

                def split(e):
                    dve.wait_ge(w_hi, e + 1)
                    part = slice(e * NW, (e + 1) * NW)
                    nc.vector.tensor_tensor(w_parts[1][:, part], w_in[:, e % 2, :], w_parts[0][:, part].bitcast(F32),
                                            ALU.subtract).then_inc(w_lo, 1)

                split(0)
                dve.wait_ge(s_w, 16 * 3)
                gate(0, 0)
                split(1)
                hidden(0, 0)

                def blockwise(n, half, last, first=False):
                    if not last:
                        ln.dve_stats(dve, n + 1, 1 - half, (n + 1) * TB)
                    dve.wait_ge(ge_ready, n + 1)
                    for e in range(E + 1):
                        if first and e + 2 <= E:
                            split(e + 2)
                        if e < E:
                            hidden(n, e + 1)
                        elif not last:
                            hidden(n + 1, 0)
                        if e == 1 and not last:
                            ln.dve_apply(dve, n + 1, 1 - half, (n + 1) * TB)
                        if e == 4 and not last:
                            lower(n + 1, 1 - half)
                        update(n, half, e)
                        if e == E and not last:
                            gate(n + 1, 1 - half)

                looped_after_first(dve, NBLK, lambda: blockwise(0, 0, False, True), blockwise)


NH = NB * H
KT = S // P
QB = S // BLK
RANK = 3
REL = 32
BAND = REL + P
SKEW = BAND + 1
NEG = -1e18
GROUP = 4
ROW = 6 * DH
VW = DH + 1
VP = 32
SCORE_BANKS = 3
MAX_BANKS = 1
MAX_SLOTS = 4
LEAD_NS = 50000


def heads_loop(eng, body):
    with eng.Fori(0, NH // 4 - 1) as it:
        for q in range(4):
            body(it * 4 + q, q, False)
    for q in range(4):
        body(NH - 4 + q, q, q == 3)


def batch(n):
    return n // (NBLK // NB)


def within(n):
    return n % (NBLK // NB)


def dram(k, name, shape, dt=F32):
    return k.nc.dram_tensor(name, shape, dt, kind="Internal").ap()


def alloc_attention(k, ctx):
    k.QD = [dram(k, f"qk_parts{m}", (RANK, NH * DH, S), BF16) for m in range(2)]
    k.ND = dram(k, "out_heads", (NH * DH, S))
    k.DD = dram(k, "denominators", (NH, S))
    k.RD = dram(k, "reciprocals", (NH, S))
    k.TD = dram(k, "rel_scores", (NH, KT, P, REL))
    k.BB = dram(k, "bias_tiles", (4, KT * P * SKEW + SKEW))
    k.PB = dram(k, "band_probs", (NH * KT, P * SKEW + 4))


def qkv_stage(k, ctx, causal):
    nc, io = k.nc, k.io
    L = int(causal)
    sem = lambda name: k.semaphore(f"qkv{L}_{name}")
    nw = 6 if causal else 4
    big = k.big
    at = [0]

    def take(n):
        at[0] += n
        return big[:, at[0] - n:at[0]]

    w = take(nw * C * D).rearrange("p (k c f) -> p k c f", k=nw, c=C)
    rr = take(2 * BLK).rearrange("p (r n) -> p r n", r=2)
    r1 = take(2 * BLK).rearrange("p (r n) -> p r n", r=2)
    parts = take(2 * RANK * BLK // 2).bitcast(BF16).rearrange("p (r t n) -> p r t n", r=2, t=RANK)
    if causal:
        cs = take(2 * S).rearrange("p (k n) -> p k n", k=2)
        ra = take(2 * BLK).rearrange("p (r n) -> p r n", r=2)
        rb = take(2 * BLK).rearrange("p (r n) -> p r n", r=2)
        relt = take(1 + REL)
        rel0, rel = relt[:, 0:1], relt[:, 1:]
        rel0row = take(D)
        hmask = take(HC)
        dbig = take(HC * REL)
        tsb = take(2 * TB * D).rearrange("p (r t n) -> p r t n", r=2, t=TB)
    ln = LayerNorm(k, sem)
    s_w = sem("weights")
    t_ready, t_free = sem("t_ready"), sem("t_free")
    u_ready = sem("u_ready")
    rr_ready = sem("rr_ready")
    p1_ready = sem("p1_ready")
    r1_ready = sem("r1_ready")
    p2_ready = sem("p2_ready")
    p3_ready = sem("p3_ready")
    s_parts = [sem(f"parts{r}") for r in range(2)]
    v_ready, v_free = sem("v_ready"), sem("v_free")
    rot = sem("rot")
    s_rel = sem("rel")
    s_t = [sem(f"t_stored{r}") for r in range(2)]
    prefilled = sem("prefilled")
    CREDIT = 2
    NU = 4
    NV = 6 if causal else 2

    W_DMAS = 5 if causal else 1

    with nc.Block() as block:
        @block.sync
        def _(sp):
            name = f"attn{L}_w"
            sp.dma_start(big[:, 0:nw * C * D], io[name][:, :]).then_inc(s_w, 16)
            if causal:
                sp.dma_start(cs[:, :, :], io["rope"][:, :, :]).then_inc(s_w, 16)
                sp.dma_start(hmask, io["hmask"][:, :]).then_inc(s_w, 16)
                sp.dma_start(relt, io["relT"][:, :]).then_inc(s_w, 16)
                row = io["rel"][0:1, :].rearrange("a d -> (a d)").unsqueeze(0).unsqueeze(0).to_broadcast([P, H, DH])
                sp.dma_start(rel0row.rearrange("p (h d) -> p h d", h=H), row).then_inc(s_w, 16)

            def store(n, u):
                kind, m, r = u // C, u % C, u % 2
                sp.wait_ge(p3_ready, n * NU + u + 1)
                dst = k.QD[kind][:, bass.ds(batch(n) * D + m * P, P), bass.ds(within(n) * BLK, BLK)]
                sp.dma_start(dst.rearrange("t p c -> p t c"), parts[:, r, :, :]).then_inc(s_parts[r], 16)

            def store_t(n, m):
                sp.wait_ge(v_free, n * NV + 2 + 2 * (m + 1) + CREDIT)
                for t in range(TB):
                    dst = k.TD[bass.ds(batch(n) * H + m * HC, HC), bass.ds(within(n) * TB + t, 1), :, :]
                    sp.dma_start(dst.rearrange("h a p j -> p (h a) j"), tsb[:, m, t, :].rearrange("p (h j) -> p h j", h=HC)).then_inc(s_t[m], 16)

            for s in s_parts + s_t:
                sp.sem_inc(s, 16)
            if causal:
                for q in range(4):
                    tiles = k.BB[q, 0:KT * P * SKEW].rearrange("(t x) -> t x", t=KT)[:, 0:P * BAND]
                    src = io["bias0"][:, 0:BAND].unsqueeze(1).to_broadcast([P, KT, BAND])
                    sp.dma_start(tiles.rearrange("t (r c) -> r t c", c=BAND), src).then_inc(prefilled, 16)
            with sp.Fori(0, NBLK) as n:
                for u in range(NU):
                    store(n, u)
                    if causal and u < C:
                        store_t(n, u)
            if causal:
                sp.wait_ge(prefilled, 16 * 4)
            for r in range(2):
                sp.wait_ge(s_parts[r], 16 * (1 + NBLK * NU // 2))
                if causal:
                    sp.wait_ge(s_t[r], 16 * (1 + NBLK * TB))

        @block.gpsimd
        def _(pool):
            pool.sem_inc(r1_ready, CREDIT)

            def blockwise(n, half, last):
                for u in range(NU):
                    r = u % 2
                    if u == 1 and not last:
                        ln.pool_rstd(pool, n + 1, 1 - half)
                    pool.wait_ge(p1_ready, n * NU + u + 1)
                    nc.gpsimd.tensor_tensor(r1[:, r, :], rr[:, r, :], parts[:, r, 0, :], ALU.subtract).then_inc(r1_ready, 1)
                    pool.wait_ge(p2_ready, n * NU + u + 1)
                    nc.gpsimd.tensor_tensor(parts[:, r, 2, :], r1[:, r, :], parts[:, r, 1, :], ALU.subtract).then_inc(p3_ready, 1)

            ln.pool_rstd(pool, 0, 0)
            looped(pool, NBLK, blockwise)

        @block.tensor
        def _(pe):
            pe.wait_ge(s_w, 16 * W_DMAS)
            if causal:
                pe.wait_ge(s_rel, 2)

            def transpose(n, half, c):
                if c == 0:
                    pe.wait_ge(ln.xn, n + 1)
                pe.wait_ge(t_free, n * C + c + 1)
                ln.pe_transpose(half, c, 6 + c).then_inc(t_ready, 1)

            def unit(n, half, u):
                kind, m, r = u // C, u % C, u % 2
                pe.wait_ge(rr_ready, n * NU + u + 1)
                for s, which in enumerate((kind, 4 + kind) if causal else (kind,)):
                    for c in range(C):
                        last = nc.tensor.matmul(k.psum[:, 2 * r + s, :], w[:, which, c, m * P:(m + 1) * P],
                                                k.xT[:, half, c, :], start=(c == 0), stop=(c == C - 1))
                last.then_inc(u_ready, 1)

            def values(n, half, pair):
                pe.wait_ge(v_free, n * NV + pair + 1)
                for t2 in range(2):
                    t = 2 * pair + t2
                    for c in range(C):
                        last = nc.tensor.matmul(k.psum[:, 4 + pair, t2 * D:(t2 + 1) * D],
                                                k.xT[:, half, c, t * P:(t + 1) * P], w[:, 2, c, :],
                                                start=(c == 0), stop=(c == C - 1))
                last.then_inc(v_ready, 1)

            def band(n, m, pair):
                if pair == 0:
                    pe.wait_ge(rr_ready, n * NU + m + 1 + CREDIT)
                pe.wait_ge(v_free, n * NV + 2 + 2 * m + pair + 1)
                for t2 in range(2):
                    t = 2 * pair + t2
                    last = nc.tensor.matmul(k.psum[:, 4 + pair, t2 * D:(t2 + 1) * D],
                                            rr[:, m, t * P:(t + 1) * P], dbig, start=True, stop=True)
                last.then_inc(v_ready, 1)

            for c in range(C):
                transpose(0, 0, c)

            def blockwise(n, half, last):
                pe.wait_ge(t_free, n * C + C + CREDIT)
                unit(n, half, 0)
                unit(n, half, 1)
                for pair in range(2):
                    values(n, half, pair)
                if causal:
                    for m in range(C):
                        for pair in range(2):
                            band(n, m, pair)
                unit(n, half, 2)
                if not last:
                    for c in range(C):
                        transpose(n + 1, 1 - half, c)
                unit(n, half, 3)

            looped(pe, NBLK, blockwise)

        @block.scalar
        def _(act):
            act.sem_inc(t_free, CREDIT)
            if not causal:
                act.sem_inc(rr_ready, CREDIT)

            def chunk(n, half, c):
                act.wait_ge(t_ready, n * C + c + 1)
                nc.scalar.copy(k.xT[:, half, c, :], k.psum[:, 6 + c, :]).then_inc(t_free, 1)

            for c in range(C):
                chunk(0, 0, c)

            def blockwise(n, half, last):
                for u in range(NU):
                    r = u % 2
                    if not causal:
                        act.wait_ge(u_ready, n * NU + u + 1)
                        act.wait_ge(r1_ready, n * NU + u + 1)
                        nc.scalar.activation(rr[:, r, :], k.psum[:, 2 * r, :], ACT.Copy,
                                             scale=D ** -0.5 if u < C else 1.0).then_inc(rr_ready, 1)
                    act.wait_ge(rr_ready, n * NU + u + 1 + CREDIT)
                    act.wait_ge(s_parts[r], (n * 2 + u // 2 + 1) * 16)
                    nc.scalar.copy(parts[:, r, 0, :], rr[:, r, :]).then_inc(p1_ready, 1)
                    act.wait_ge(r1_ready, n * NU + u + 1 + CREDIT)
                    nc.scalar.copy(parts[:, r, 1, :], r1[:, r, :]).then_inc(p2_ready, 1)
                    if u >= 2 and not last:
                        chunk(n + 1, 1 - half, u - 2)

            looped(act, NBLK, blockwise)

        @block.vector
        def _(dve):
            dve.sem_inc(v_free, CREDIT)
            if causal:
                dve.sem_inc(rr_ready, CREDIT)
                dve.wait_ge(s_w, 16 * W_DMAS)
                nc.vector.tensor_scalar(rel, rel, rel0, None, ALU.subtract).then_inc(s_rel, 1)
                dve.wait_ge(s_rel, 1)
                nc.vector.tensor_tensor(dbig.rearrange("p (h j) -> p h j", h=HC),
                                        rel.unsqueeze(1).to_broadcast([P, HC, REL]),
                                        hmask.unsqueeze(2).to_broadcast([P, HC, REL]), ALU.mult).then_inc(s_rel, 1)
            ln.dve_stats(dve, 0, 0, 0)
            ln.dve_apply(dve, 0, 0, 0)

            def rotate(n, u):
                kind, r = u // C, u % 2
                cols = bass.ds(within(n) * BLK, BLK)
                scale = DH ** -0.5 if kind == 0 else 1.0
                dve.wait_ge(u_ready, n * NU + u + 1)
                dve.wait_ge(r1_ready, n * NU + u + 1)
                if u >= C:
                    dve.wait_ge(v_ready, n * NV + 2 + 2 * (u - C + 1))
                nc.vector.scalar_tensor_tensor(ra[:, r, :], k.psum[:, 2 * r, :], scale, cs[:, 0, cols],
                                               ALU.mult, ALU.mult)
                nc.vector.scalar_tensor_tensor(rb[:, r, :], k.psum[:, 2 * r + 1, :], scale, cs[:, 1, cols],
                                               ALU.mult, ALU.mult).then_inc(rot, 1)
                dve.wait_ge(rot, n * NU + u + 1)
                nc.vector.scalar_tensor_tensor(rr[:, r, :], ra[:, r, :], rel0 if kind else 0.0, rb[:, r, :],
                                               ALU.add, ALU.add).then_inc(rr_ready, 1)

            def values(n, pair):
                dve.wait_ge(v_ready, n * NV + pair + 1)
                src = k.psum[:, 4 + pair, :].rearrange("p (t h d) -> p t h d", t=2, h=H)
                for t2 in range(2):
                    dst = k.V[:, bass.ds(batch(n), 1), :, bass.ds(within(n) * TB + 2 * pair + t2, 1), :]
                    dst = dst.rearrange("p a h b d -> p (a h b) d")
                    if causal:
                        last = nc.vector.tensor_tensor(dst, src[:, t2], rel0row.rearrange("p (h d) -> p h d", h=H), ALU.add)
                    else:
                        last = nc.vector.tensor_copy(dst, src[:, t2])
                last.then_inc(v_free, 1)

            def band(n, m, pair):
                if pair == 0:
                    dve.wait_ge(s_t[m], (n * TB + 1) * 16)
                dve.wait_ge(v_ready, n * NV + 2 + 2 * m + pair + 1)
                nc.vector.tensor_copy(tsb[:, m, 2 * pair:2 * pair + 2, :],
                                      k.psum[:, 4 + pair, :].rearrange("p (t n) -> p t n", t=2)).then_inc(v_free, 1)

            def blockwise(n, half, last):
                if not last:
                    ln.dve_stats(dve, n + 1, 1 - half, (n + 1) * TB)
                if causal:
                    rotate(n, 0)
                    rotate(n, 1)
                for pair in range(2):
                    values(n, pair)
                if not last:
                    ln.dve_apply(dve, n + 1, 1 - half, (n + 1) * TB)
                if causal:
                    for m in range(C):
                        for pair in range(2):
                            band(n, m, pair)
                    rotate(n, 2)
                    rotate(n, 3)

            looped(dve, NBLK, blockwise)


def score_units(causal, kt):
    first = kt * P if causal else 0
    return [(j, max(first, j * BLK), (j + 1) * BLK) for j in range(QB) if (j + 1) * BLK > first]


def max_units(causal, t):
    wide = MAX_BANKS * BLK
    end = t * P - REL if causal else S
    far = [("far", lo, min(lo + wide, end), lo // wide) for lo in range(0, max(end, 0), wide)]
    return [("band", t * P - REL, (t + 1) * P, QB // MAX_BANKS)] * causal + far


def max_ring(causal):
    out = []
    for t in range(KT):
        out += [(t, u) for u in max_units(causal, t)]
        if t % GROUP == 1 and t > 1:
            out.append((t, ("row", t // GROUP - 1, 0, 0)))
    out.append((KT - 1, ("row", KT // GROUP - 1, 0, 0)))
    return out


def tensor_order(causal, ring):
    fixed, late = 100, 100
    exp = lambda w: fixed + 0.75 * w
    reduce = lambda w: fixed / 2 + 1.04 * w
    cost = {"far": reduce, "band": lambda w: 4 * fixed + 2 * w, "row": lambda w: 4 * fixed}
    scores = [(kt, n, hi - lo) for kt in range(KT) for n, (_, lo, hi) in enumerate(score_units(causal, kt))]
    maxima = [(kind, hi - lo) for _, (kind, lo, hi, _) in ring[:-1]]
    order = [("score", 0, 0), ("last row", len(ring) - 1, 0)]
    pe = act = dve = 0.0
    exps, reduced, sums = [exp(BLK)], [], 0.0
    act, pe = exps[0], 500.0
    waiting = []
    exp_all, exp_done = sum(exp(w) for _, _, w in scores), exp(BLK)
    dve_all, dve_done = sum(cost[kind](w) for kind, w in maxima), 0.0
    u = 1
    while u < len(scores) or len(reduced) < len(maxima):
        m = len(reduced)
        s_start = m_start = float("inf")
        if u < len(scores):
            s_start = max(pe, exps[u - SCORE_BANKS] if u >= SCORE_BANKS else 0.0)
        if m < len(maxima):
            m_start = max(pe, reduced[m - MAX_SLOTS] if m >= MAX_SLOTS else 0.0)
            if maxima[m][0] == "row":
                m_start = max(m_start, sums)
        lead = exp_done / exp_all - dve_done / dve_all
        if s_start + LEAD_NS * lead < m_start or m == len(maxima):
            kt, n, w = scores[u]
            order.append(("score", kt, n))
            pe = s_start + 0.43 * w + fixed * causal
            act = max(act, pe + late) + exp(w)
            exps.append(act + late)
            exp_done += exp(w)
            if u + 1 == len(scores) or scores[u + 1][0] != kt:
                waiting.append((u + SCORE_BANKS, kt))
            if waiting and waiting[0][0] <= u:
                kt = waiting.pop(0)[1]
                order.append(("values", kt, 0))
                pe += 0.48 * sum(w for at, _, w in scores if at == kt)
            u += 1
        else:
            kind, w = maxima[m]
            order.append(("max", m, 0))
            pe = m_start + (0.43 * w if kind != "row" else 3 * fixed)
            dve = max(dve, pe + late) + cost[kind](w)
            reduced.append(dve + late)
            dve_done += cost[kind](w)
            if kind == "band":
                sums = dve + 4 * fixed
            m += 1
    return order + [("values", kt, 0) for _, kt in waiting]


def heads_stage(k, ctx, causal):
    nc, io = k.nc, k.io
    L = int(causal)
    sem = lambda name: k.semaphore(f"heads{L}_{name}")
    big = k.big
    at = [0]

    def take(n, dt=F32):
        at[0] += n
        v = big[:, at[0] - n:at[0]]
        return v.bitcast(dt) if dt != F32 else v

    MS = QB // MAX_BANKS + causal
    q_sb = take(4 * S // 2, BF16).rearrange("p (r n) -> p r n", r=4)
    k_sb = take(4 * S // 2, BF16).rearrange("p (r n) -> p r n", r=4)
    pT = take(4 * S).rearrange("p (r n) -> p r n", r=4)
    vh = take(2 * KT * VP).rearrange("p (r t d) -> p r t d", r=2, t=KT)
    osb = take(2 * BLK).rearrange("p (r n) -> p r n", r=2)
    mx = take(2 * KT * MS).rearrange("p (r t s) -> p r t s", r=2, t=KT)
    mm = take(2 * KT).rearrange("p (r t) -> p r t", r=2)
    nm = take(2 * KT // 2, BF16).rearrange("p (r t) -> p r t", r=2)
    identb = take(P // 2, BF16)
    if causal:
        bt = k.arena[:, 0:4 * KT * BAND].rearrange("p (r t c) -> p r t c", r=4, t=KT)
        sb = [buf[:, :, :, :].rearrange("p a b c -> p (a b c)")[:, 0:KT // 2 * BAND].rearrange("p (t c) -> p t c", c=BAND)
              for buf in (k.xn, k.xT)]
        band_group = lambda g: sb[g * GROUP // (KT // 2)][:, g * GROUP % (KT // 2):g * GROUP % (KT // 2) + GROUP, :]
        band_of = lambda t: sb[t // (KT // 2)][:, t % (KT // 2), :]

    SU = [score_units(causal, kt) for kt in range(KT)]
    S_BEFORE = [sum(len(x) for x in SU[:kt]) for kt in range(KT + 1)]
    NS = S_BEFORE[KT]
    RING = max_ring(causal)
    NM = len(RING)
    ORDER = tensor_order(causal, RING)
    ROWS_AT = [n for n, (_, u) in enumerate(RING) if u[0] == "row"]
    AFTER_ROW = [next((o[1:] for o in ORDER[ORDER.index(("max", n, 0)):] if o[0] == "score")) for n in ROWS_AT[:-1]]
    LOADS = 6 + 3
    NG = KT // GROUP
    PC = 4096
    PVC = 4 * KT
    M_BEFORE = [sum(u[0] != "row" for _, u in RING[:n]) for n in range(NM + 1)]
    NX = M_BEFORE[NM]
    assert NM % MAX_SLOTS == 0

    qk_loaded = [sem(f"qk_loaded{q}") for q in range(4)]
    bt_loaded = [sem(f"bt_loaded{q}") for q in range(4)]
    skewed = [sem(f"skewed{q}") for q in range(4)]
    const = sem("const")
    s_ready = sem("s_ready")
    p_ready = sem("p_ready")
    pv_done = sem("pv_done")
    m_ready = sem("m_ready")
    m_free = sem("m_free")
    row_done = sem("row_done")
    band_max = sem("band_max")
    mm_ready = sem("mm_ready")
    nm_ready = sem("nm_ready")
    pb_ready = sem("pb_ready")
    pb_stored = [sem(f"pb_stored{g}") for g in range(NG)]
    vh_ready = sem("vh_ready")
    o_free = sem("o_free")
    o_stored = [sem(f"o_stored{r}") for r in range(2)]

    def band_cols(t):
        return (REL if t == 0 else 0), BAND

    with nc.Block() as block:
        @block.sync
        def _(sp):
            def load(i, q, turn):
                sp.wait_ge(pv_done, i * KT + KT)
                rows = bass.ds(i * DH, DH)
                at = 0
                for part, n in ((0, 3), (1, 2), (2, 1)):
                    for _ in range(n):
                        sp.dma_start(q_sb[at:at + DH, q, :], k.QD[0][part, rows, :]).then_inc(qk_loaded[q], 16)
                        at += DH
                at = 0
                for n in (3, 2, 1):
                    sp.dma_start(k_sb[at:at + n * DH, q, :], k.QD[1][0:n, rows, :]).then_inc(qk_loaded[q], 16)
                    at += n * DH
                if causal:
                    diag = k.BB[q, 1:1 + KT * P * SKEW].rearrange("(r c) -> r c", c=SKEW)[:, 0:REL]
                    src = k.TD[bass.ds(i, 1), :, :, :].rearrange("a t r j -> (a t r) j")
                    sp.dma_start(diag, src).then_inc(skewed[q], 16)
                    sp.wait_ge(skewed[q], 16 * (turn + 1))
                    slot = k.BB[q, 0:KT * P * SKEW].rearrange("(t x) -> t x", t=KT)[:, 0:P * BAND]
                    sp.dma_start(bt[:, q, :, :], slot.rearrange("t (r c) -> r t c", c=BAND)).then_inc(bt_loaded[q], 16)

            def store(j, r):
                sp.wait_ge(o_free, j + 2)
                for b in range(QB):
                    cols = slice(b * BLK, (b + 1) * BLK)
                    sp.dma_start(k.ND[bass.ds(j * DH, DH), cols], osb[32 * b:32 * b + DH, r, :]).then_inc(o_stored[r], 16)
                    sp.dma_start(k.DD[bass.ds(j, 1), cols], osb[32 * b + DH:32 * b + VW, r, :]).then_inc(o_stored[r], 16)

            for r in range(2):
                sp.sem_inc(o_stored[r], 16)
            for q in range(4):
                load(q, q, 0)
            with sp.Fori(1, NH // 4) as it:
                for q in range(4):
                    load(it * 4 + q, q, it)
                    store((it - 1) * 4 + q, q % 2)
            for q in range(4):
                store(NH - 4 + q, q % 2)
            for r in range(2):
                sp.wait_ge(o_stored[r], 16 * (1 + 2 * QB * NH // 2))

        @block.gpsimd
        def _(pool):
            def store_band(i, g):
                pool.wait_ge(pb_ready, i * NG + g + 1)
                dst = k.PB[bass.ds(i * KT + g * GROUP, GROUP), 0:P * BAND].rearrange("t (r c) -> r t c", c=BAND)
                pool.dma_start(dst, band_group(g)).then_inc(pb_stored[g], 16)

            def gather(i, q):
                pool.wait_ge(pv_done, PVC + (i - 1) * KT)
                src = k.V[:, bass.ds(i // H, 1), bass.ds(i % H, 1), :, :].rearrange("p a b t d -> p (a b t) d")
                nc.gpsimd.tensor_copy(vh[:, q % 2, :, 0:DH], src).then_inc(vh_ready, 1)

            pool.wait_ge(const, 1)
            if causal:
                for g in range(NG - 1):
                    store_band(0, g)

            def body(i, q, last):
                gather(i, q)
                if causal:
                    store_band(i, NG - 1)
                    if not last:
                        for g in range(NG - 1):
                            store_band(i + 1, g)

            heads_loop(pool, body)
            if causal:
                for g in range(NG):
                    pool.wait_ge(pb_stored[g], 16 * NH)

        @block.tensor
        def _(pe):
            def scores(i, q, kt, n):
                u = S_BEFORE[kt] + n
                j, lo, hi = SU[kt][n]
                bank = 4 + u % SCORE_BANKS
                if u >= SCORE_BANKS:
                    pe.wait_ge(p_ready, PC + i * NS + u + 1 - SCORE_BANKS)
                else:
                    former = max(v for v in range(NS) if v % SCORE_BANKS == u)
                    pe.wait_ge(p_ready, PC - NS + i * NS + former + 1)
                if kt == 0:
                    pe.wait_ge(row_done, NG + i * NG + j + 1)
                last = nc.tensor.matmul(k.psum[:, bank, 0:hi - lo], k_sb[0:ROW + 1, q, kt * P:(kt + 1) * P],
                                        q_sb[0:ROW + 1, q, lo:hi], start=True, stop=not causal, skip_group_check=causal)
                if causal and lo <= kt * P < hi:
                    at = kt * P - lo
                    last = nc.tensor.matmul(k.psum[:, bank, at:at + P], bt[:, q, kt, REL:BAND], k.ident[:, :],
                                            start=False, stop=True, skip_group_check=True)
                if causal and lo <= (kt + 1) * P < hi:
                    at = (kt + 1) * P - lo
                    last = nc.tensor.matmul(k.psum[P - REL:P, bank, at:at + REL], bt[:, q, kt + 1, 0:REL],
                                            k.ident[:, 0:REL], start=False, stop=True, skip_group_check=True)
                last.then_inc(s_ready, 1)

            def weighted(i, q, kt):
                pe.wait_ge(p_ready, PC + i * NS + S_BEFORE[kt + 1])
                if kt == 0:
                    pe.wait_ge(vh_ready, i + 1)
                    pe.wait_ge(o_free, i + 1)
                for j, lo, hi in SU[kt]:
                    last = nc.tensor.matmul(k.psum[32 * j:32 * j + VP, 7, lo - j * BLK:hi - j * BLK],
                                            vh[:, q % 2, kt, :], pT[:, kt % 4, lo:hi],
                                            start=(kt == 0), stop=(kt == KT - 1), skip_group_check=True)
                last.then_inc(pv_done, 1)

            def maxima(i, q, idx):
                t, (kind, lo, hi, slot) = RING[idx]
                b = MAX_BANKS * (idx % MAX_SLOTS)
                former = idx - MAX_SLOTS if idx >= MAX_SLOTS else idx - MAX_SLOTS + NM
                turn = NX if idx >= MAX_SLOTS else 0
                if RING[former][1][0] == "row":
                    pe.wait_ge(row_done, i * NG + (NG if turn else 0) + former + 1 - M_BEFORE[former])
                else:
                    pe.wait_ge(m_free, i * NX + turn + M_BEFORE[former] + 1)
                if kind == "far":
                    for c in range(lo, hi, BLK):
                        e = min(c + BLK, hi)
                        last = nc.tensor.matmul(k.psum[:, b + (c - lo) // BLK, 0:e - c],
                                                q_sb[0:ROW, q, t * P:(t + 1) * P], k_sb[0:ROW, q, c:e],
                                                start=True, stop=True)
                elif kind == "band":
                    c0, c1 = band_cols(t)
                    last = nc.tensor.matmul(k.psum[:, b, c0:c1], q_sb[0:ROW, q, t * P:(t + 1) * P],
                                            k_sb[0:ROW, q, lo + c0:hi], start=True, stop=True)
                else:
                    pe.wait_ge(nm_ready, i * NG + lo + 1)
                    for n in range(GROUP):
                        last = nc.tensor.matmul(k.psum[ROW:ROW + 1, b, n * P:(n + 1) * P],
                                                nm[:, q % 2, lo * GROUP + n:lo * GROUP + n + 1], identb[:, :],
                                                start=True, stop=True)
                last.then_inc(m_ready, 1)

            def arrived(i, q):
                pe.wait_ge(qk_loaded[q], 16 * LOADS * (i // 4 + 1))
                if causal:
                    pe.wait_ge(bt_loaded[q], 16 * (i // 4 + 1))

            pe.wait_ge(const, 3)
            arrived(0, 0)
            for idx in range(NM - 1):
                maxima(0, 0, idx)

            def body(i, q, last):
                if not last:
                    arrived(i + 1, (q + 1) % 4)
                for what, a, n in ORDER:
                    if what == "score":
                        scores(i, q, a, n)
                    elif what == "values":
                        weighted(i, q, a)
                    elif what == "last row":
                        maxima(i, q, a)
                    elif not last:
                        maxima(i + 1, (q + 1) % 4, a)

            heads_loop(pe, body)

        @block.scalar
        def _(act):
            act.sem_inc(p_ready, PC)

            def band_exp(i, q, g):
                act.wait_ge(nm_ready, i * NG + g + 1)
                for t in range(g * GROUP, (g + 1) * GROUP):
                    c0, c1 = band_cols(t)
                    last = nc.scalar.activation(band_of(t)[:, c0:c1], band_of(t)[:, c0:c1], ACT.Exp,
                                                bias=nm[:, q % 2, t:t + 1])
                last.then_inc(pb_ready, 1)

            def row(i, q, g):
                idx = ROWS_AT[g]
                act.wait_ge(m_ready, i * NM + idx + 1)
                nc.scalar.copy(q_sb[ROW:ROW + 1, q, g * BLK:(g + 1) * BLK],
                               k.psum[ROW:ROW + 1, MAX_BANKS * (idx % MAX_SLOTS), :]).then_inc(row_done, 1)

            for g in range(NG - 1):
                row(0, 0, g)
                if causal:
                    band_exp(0, 0, g)

            def body(i, q, last):
                for kt in range(KT):
                    act.wait_ge(pv_done, PVC + i * KT + kt - 3)
                    for n, (j, lo, hi) in enumerate(SU[kt]):
                        u = S_BEFORE[kt] + n
                        act.wait_ge(s_ready, i * NS + u + 1)
                        nc.scalar.activation(pT[:, kt % 4, lo:hi], k.psum[:, 4 + u % SCORE_BANKS, 0:hi - lo],
                                             ACT.Exp).then_inc(p_ready, 1)
                        if (kt, n) == (0, 0):
                            row(i, q, NG - 1)
                        if causal and (kt, n) == (0, 2):
                            band_exp(i, q, NG - 1)
                        if not last and (kt, n) in AFTER_ROW:
                            row(i + 1, (q + 1) % 4, AFTER_ROW.index((kt, n)))
                            if causal:
                                band_exp(i + 1, (q + 1) % 4, AFTER_ROW.index((kt, n)))

            heads_loop(act, body)

        @block.vector
        def _(dve):
            dve.sem_inc(pv_done, PVC)
            dve.sem_inc(m_free, NX)
            dve.sem_inc(row_done, NG)
            dve.sem_inc(o_free, 1)
            nc.vector.memset(vh[:, :, :, DH + 1:VP], 0.0)
            nc.vector.memset(vh[:, :, :, DH:DH + 1], 1.0).then_inc(const, 1)
            nc.vector.memset(mx[:, :, :, :], -3e38)
            nc.vector.memset(k_sb[ROW:ROW + 1, :, :], 1.0).then_inc(const, 1)
            nc.vector.tensor_copy(identb, k.ident[:, :]).then_inc(const, 1)
            if causal:
                nc.vector.memset(band_of(0)[:, 0:REL], 0.0).then_inc(const, 1)
            dve.wait_ge(const, 3 + L)

            def maxima(i, q, idx, first=False):
                t, (kind, lo, hi, slot) = RING[idx]
                r, b = q % 2, MAX_BANKS * (idx % MAX_SLOTS)
                if kind == "row":
                    return
                dve.wait_ge(m_ready, i * NM + idx + 1)
                if kind == "far":
                    src = k.psum[:, b:b + MAX_BANKS, :].rearrange("p b n -> p (b n)")[:, 0:hi - lo]
                    nc.vector.reduce_max(mx[:, r, t, slot:slot + 1], src, AX_X).then_inc(m_free, 1)
                else:
                    c0, c1 = band_cols(t)
                    dve.wait_ge(bt_loaded[q], 16 * (i // 4 + 1))
                    if not first:
                        dve.wait_ge(pb_stored[t // GROUP], 16 * i)
                    nc.vector.tensor_tensor(band_of(t)[:, c0:c1], k.psum[:, b, c0:c1], bt[:, q, t, c0:c1],
                                            ALU.add).then_inc(m_free, 1)
                if causal and (t == 0 or slot == 0):
                    c0, c1 = band_cols(t)
                    dve.wait_ge(m_free, NX + i * NX + M_BEFORE[idx] + (t == 0))
                    nc.vector.reduce_max(mx[:, r, t, MS - 1:MS], band_of(t)[:, c0:c1], AX_X).then_inc(band_max, 1)
                if RING[idx + 1][0] != t or RING[idx + 1][1][0] == "row":
                    if t % GROUP == GROUP - 1:
                        g = t // GROUP
                        ts = slice(g * GROUP, (g + 1) * GROUP)
                        dve.wait_ge(m_free, NX + i * NX + M_BEFORE[idx + 1])
                        if causal:
                            dve.wait_ge(band_max, i * KT + t + 1)
                        nc.vector.reduce_max(mm[:, r, ts], mx[:, r, ts, :], AX_X).then_inc(mm_ready, 1)
                        dve.wait_ge(mm_ready, i * NG + g + 1)
                        nc.vector.tensor_scalar(nm[:, r, ts], mm[:, r, ts], -1.0, None, ALU.mult).then_inc(nm_ready, 1)

            for idx in range(NM - 1):
                maxima(0, 0, idx, first=True)

            def body(i, q, last):
                if not last:
                    for idx in range(NM - 1):
                        maxima(i + 1, (q + 1) % 4, idx)
                dve.wait_ge(pv_done, PVC + (i + 1) * KT)
                dve.wait_ge(o_stored[q % 2], 16 * (1 + 2 * QB * (i // 2)))
                nc.vector.tensor_copy(osb[:, q % 2, :], k.psum[:, 7, :]).then_inc(o_free, 1)

            heads_loop(dve, body)


def project_stage(k, ctx, causal):
    nc, io = k.nc, k.io
    L = int(causal)
    sem = lambda name: k.semaphore(f"proj{L}_{name}")
    big = k.big
    at = [0]

    def take(n):
        at[0] += n
        return big[:, at[0] - n:at[0]]

    w = take(C * D).rearrange("p (c f) -> p c f", c=C)
    num = take(2 * C * BLK).rearrange("p (r c n) -> p r c n", r=2, c=C)
    rd = take(2 * C * BLK).rearrange("p (r c n) -> p r c n", r=2, c=C)
    o = take(2 * C * BLK).rearrange("p (r c n) -> p r c n", r=2, c=C)
    rec = take(BLK)
    bias = take(D)
    spread = take(P)
    if causal:
        wt = take(2 * H * REL).rearrange("p (r n) -> p r n", r=2)
        wT = take(H * REL // P * BLK).rearrange("p (g n) -> p g n", n=BLK)
        sm = take(C * BLK).rearrange("p (c n) -> p c n", c=C)
        rel = take(DH)
        rel0 = take(DH)
        jmask = take(GROUP)
        dbig = take(GROUP * DH)
    s_w, s_rec, s_rc = sem("weights"), sem("recip_dma"), sem("recip")
    s_ld = [sem(f"loaded{r}") for r in range(2)]
    s_wt = [sem(f"band_loaded{r}") for r in range(2)]
    rb_ready = sem("rb_ready")
    o_ready = sem("o_ready")
    y_ready = sem("y_ready")
    y_free = sem("y_free")
    s_b = sem("bias_added")
    tp_ready = sem("tp_ready")
    tp_free = sem("tp_free")
    ex_ready = sem("ex_ready")
    ex_done = sem("ex_done")
    s_rel = sem("rel")
    W_DMAS = 2 + (GROUP + 2 if causal else 1)
    NGR = H // GROUP

    with nc.Block() as block:
        @block.sync
        def _(sp):
            wv = io[f"attn{L}_w"].rearrange("p (k x) -> p k x", x=C * D)
            sp.dma_start(big[:, 0:C * D], wv[:, 3, :]).then_inc(s_w, 16)
            sp.dma_start(spread[0:HC, :], io["spread"][:, :]).then_inc(s_w, 16)
            if causal:
                for g in range(GROUP):
                    sp.dma_start(rel[g * REL:(g + 1) * REL, :], io["rel"][1:1 + REL, :]).then_inc(s_w, 16)
                sp.dma_start(rel0, io["rel"][0:1, :].to_broadcast([P, DH])).then_inc(s_w, 16)
                sp.dma_start(jmask, io["jmask"][:, :]).then_inc(s_w, 16)
            else:
                sp.dma_start(bias, io["bff"][0:1, :].to_broadcast([P, D])).then_inc(s_w, 16)
            sp.dma_start(rec, k.DD.rearrange("i (b c) -> (i b) c", b=QB)).then_inc(s_rec, 16)
            sp.wait_ge(s_rc, 1)
            sp.dma_start(k.RD.rearrange("i (b c) -> (i b) c", b=QB), rec).then_inc(s_rec, 16)
            sp.wait_ge(s_rec, 32)

            def load(n, half):
                sp.wait_ge(o_ready, (n + 1) * C)
                cols = bass.ds(within(n) * BLK, BLK)
                src = k.ND[bass.ds(batch(n) * D, D), cols]
                sp.dma_start(num[:, half, :, :], src.rearrange("(c p) n -> p c n", p=P)).then_inc(s_ld[half], 16)
                src = k.RD[bass.ds(batch(n) * H, H), cols]
                sp.dma_start(rd[0:HC, half, :, :], src.rearrange("(c h) n -> h c n", h=HC)).then_inc(s_ld[half], 16)
                if causal:
                    for t in range(TB):
                        sp.wait_ge(tp_ready, n * TB + t + 1)
                        tile = bass.DynSlice(batch(n) * H * KT + within(n) * TB + t, H, KT)
                        src = k.PB[tile, 1:1 + P * SKEW].rearrange("h (r c) -> r h c", c=SKEW)[:, :, 0:REL]
                        sp.dma_start(wt[:, t % 2, :].rearrange("p (h j) -> p h j", h=H), src).then_inc(s_wt[t % 2], 16)

            with sp.Fori(0, NBLK // 2) as it:
                for half in range(2):
                    load(it * 2 + half, half)

        @block.tensor
        def _(pe):
            pe.sem_inc(y_ready, 4)
            pe.wait_ge(s_w, 16 * W_DMAS)
            if causal:
                pe.sem_inc(ex_ready, C)
            if causal:
                pe.wait_ge(s_rel, 2)

            def blockwise(n, half, last):
                if causal:
                    for t in range(TB):
                        pe.wait_ge(s_wt[t % 2], 16 * (n * 2 + t // 2 + 1))
                        pe.wait_ge(tp_free, n * TB + t + 1)
                        for g in range(NGR):
                            last_mm = nc.tensor.transpose(k.psum[:, 6 + t % 2, g * P:(g + 1) * P],
                                                          wt[:, t % 2, g * P:(g + 1) * P], k.ident[:, :])
                        last_mm.then_inc(tp_ready, 1)
                    pe.wait_ge(tp_free, 2 + (n + 1) * TB)
                    for c in range(C):
                        pe.wait_ge(o_ready, 2 * C + (n - 1) * C + c + 1)
                        for g2 in range(2):
                            last_mm = nc.tensor.matmul(k.psum[64 * g2:64 * (g2 + 1), 2 + c, :], dbig,
                                                       wT[:, 2 * c + g2, :], start=True, stop=True)
                        last_mm.then_inc(ex_ready, 1)
                pe.wait_ge(s_ld[half], 32 * (n // 2 + 1))
                for c in range(C):
                    pe.wait_ge(o_ready, 2 * C + (n - 1) * C + c + 1)
                    nc.tensor.matmul(k.psum[:, c, :], spread[0:HC, :], rd[0:HC, half, c, :],
                                     start=True, stop=True).then_inc(rb_ready, 1)
                pe.wait_ge(o_ready, 2 * C + (n + 1) * C)
                for pair in range(2):
                    pe.wait_ge(y_free, n * 2 + pair + 1)
                    for t2 in range(2):
                        t = 2 * pair + t2
                        for c in range(C):
                            last_mm = nc.tensor.matmul(k.psum[:, 4 + pair, t2 * D:(t2 + 1) * D],
                                                       o[:, half, c, t * P:(t + 1) * P], w[:, c, :],
                                                       start=(c == 0), stop=(c == C - 1))
                    last_mm.then_inc(y_ready, 1)

            looped(pe, NBLK, blockwise)

        @block.scalar
        def _(act):
            if causal:
                act.sem_inc(tp_free, 2)

                def blockwise(n, half, last):
                    for t in range(TB):
                        act.wait_ge(tp_ready, 2 + n * TB + t + 1)
                        act.wait_ge(ex_ready, C + n * C)
                        nc.scalar.copy(wT[:, :, t * P:(t + 1) * P],
                                       k.psum[:, 6 + t % 2, :].rearrange("p (g n) -> p g n", n=P)).then_inc(tp_free, 1)

                looped(act, NBLK, blockwise)

        @block.vector
        def _(dve):
            dve.sem_inc(o_ready, 2 * C)
            dve.sem_inc(y_free, 2)
            dve.wait_ge(s_rec, 16)
            nc.vector.reciprocal(rec, rec).then_inc(s_rc, 1)
            dve.wait_ge(s_w, 16 * W_DMAS)
            if causal:
                dve.sem_inc(tp_ready, 2)
                nc.vector.tensor_tensor(rel, rel, rel0, ALU.subtract).then_inc(s_rel, 1)
                dve.wait_ge(s_rel, 1)
                nc.vector.tensor_tensor(dbig.rearrange("p (h d) -> p h d", h=GROUP),
                                        rel.unsqueeze(1).to_broadcast([P, GROUP, DH]),
                                        jmask.unsqueeze(2).to_broadcast([P, GROUP, DH]), ALU.mult).then_inc(s_rel, 1)

            def blockwise(n, half, last):
                dve.wait_ge(s_ld[half], 32 * (n // 2 + 1))
                for c in range(C):
                    src = num[:, half, c, :]
                    if causal:
                        dve.wait_ge(ex_ready, C + n * C + c + 1)
                        nc.vector.tensor_tensor(sm[:, c, :], k.psum[:, 2 + c, :], src, ALU.add).then_inc(ex_done, 1)
                        dve.wait_ge(ex_done, n * C + c + 1)
                        src = sm[:, c, :]
                    dve.wait_ge(rb_ready, n * C + c + 1)
                    if c == 0:
                        dve.wait_ge(y_ready, 4 + (n - 1) * 2)
                    nc.vector.tensor_tensor(o[:, half, c, :], k.psum[:, c, :], src, ALU.mult).then_inc(o_ready, 1)
                for pair in range(2):
                    tiles = k.X[:, bass.ds(n * TB + 2 * pair, 2), :]
                    if not causal:
                        nc.vector.tensor_tensor(tiles, tiles, bias.unsqueeze(1).to_broadcast([P, 2, D]),
                                                ALU.add).then_inc(s_b, 1)
                        dve.wait_ge(s_b, n * 2 + pair + 1)
                    dve.wait_ge(y_ready, 4 + n * 2 + pair + 1)
                    nc.vector.tensor_tensor(tiles, k.psum[:, 4 + pair, :].rearrange("p (t n) -> p t n", t=2), tiles,
                                            ALU.add).then_inc(y_free, 1)

            looped(dve, NBLK, blockwise)


def lstm_stage(k, ctx, run):
    nc, io = k.nc, k.io
    sem = lambda name: k.semaphore(f"lstm{run}_{name}")
    big = k.big
    at = [0]

    def take(n):
        at[0] += n
        return big[:, at[0] - n:at[0]]

    w = k.arena[:, 0:8 * C * D].rearrange("p (k c f) -> p k c f", k=8, c=C)
    xT = take(2 * 2 * C * BLK).rearrange("p (r t c n) -> p r t c n", r=2, t=2, c=C)
    gates = take(2 * 3 * C * BLK).rearrange("p (s g c n) -> p s g c n", s=2, g=3, c=C)
    ig = take(C * BLK).rearrange("p (c n) -> p c n", c=C)
    cell = take(2 * C * BLK).rearrange("p (s c n) -> p s c n", s=2, c=C)
    fc = take(C * BLK).rearrange("p (c n) -> p c n", c=C)
    pre = take(2 * BLK).rearrange("p (r n) -> p r n", r=2)
    th = take(2 * BLK).rearrange("p (r n) -> p r n", r=2)
    b = take(4 * C).rearrange("p (k c) -> p k c", k=4)
    b0 = take(3 * C).rearrange("p (k c) -> p k c", k=3)
    bo = take(D)
    NBK = S // BLK
    NU = 3 * C
    NO = 2 * TB // 2
    NT = 2 * C

    ln = LayerNorm(k, sem)
    s_w, s_b0 = sem("weights"), sem("b0")
    t_ready, t_free = sem("t_ready"), sem("t_free")
    g_ready = sem("g_ready")
    g_done = sem("g_done")
    ig_done = sem("ig_done")
    c_ready = sem("c_ready")
    o_ready = sem("o_ready")
    pre_done = sem("pre_done")
    th_done = sem("th_done")
    x_done = sem("x_done")

    with nc.Block() as block:
        @block.sync
        def _(sp):
            sp.dma_start(k.arena[:, 0:8 * C * D], io["lstm_w"][:, :]).then_inc(s_w, 16)
            sp.dma_start(b, io["lstm_b"][:, :, :]).then_inc(s_w, 16)
            sp.dma_start(bo, io["bo"][0:1, :].to_broadcast([P, D])).then_inc(s_w, 16)

        @block.gpsimd
        def _(pool):
            def both(m):
                for t in range(2):
                    ln.pool_rstd(pool, m + t, t)

            both(0)
            with pool.Fori(1, NBK) as n:
                both(n * 2)

        @block.tensor
        def _(pe):
            def transposes(n, first=False):
                for i in range(NT):
                    t, c = i // C, i % C
                    if c == 0:
                        pe.wait_ge(ln.xn, n * 2 + t + 1)
                    if i == 0 and not first:
                        pe.wait_ge(pre_done, (n - 1) * NO + 2)
                    pe.wait_ge(t_free, n * NT + i + 1)
                    ln.pe_transpose(t, c, 6 + c).then_inc(t_ready, 1)

            pe.wait_ge(s_w, 16 * 3)
            for g in range(3):
                for m in range(C):
                    for c in range(C):
                        last_mm = nc.tensor.matmul(k.psum[:, 5, g * C + m:g * C + m + 1],
                                                   w[:, 2 * g + 1, c, m * P:(m + 1) * P], b[:, 3, c:c + 1],
                                                   start=(c == 0), stop=(c == C - 1))
            last_mm.then_inc(s_b0, 1)
            pe.wait_ge(s_b0, 2)
            transposes(0, first=True)

            def blockwise(n, r, last):
                pe.wait_ge(t_free, 2 + (n + 1) * NT)
                for u in range(NU):
                    g, m = u // C, u % C
                    pe.wait_ge(g_done, n * 2 * NU + u + 1)
                    for c in range(C):
                        last_mm = nc.tensor.matmul(k.psum[:, u, :], w[:, 2 * g, c, m * P:(m + 1) * P],
                                                   xT[:, r, 0, c, :], start=(c == 0), stop=(c == C - 1))
                    last_mm.then_inc(g_ready, 1)
                for u in range(NU):
                    g, m = u // C, u % C
                    pe.wait_ge(g_done, n * 2 * NU + NU + u + 1)
                    for c in range(C):
                        nc.tensor.matmul(k.psum[:, u, :], w[:, 2 * g, c, m * P:(m + 1) * P],
                                         xT[:, r, 1, c, :], start=(c == 0), stop=False)
                pe.wait_ge(c_ready, n * 2 * C + C)
                for u in range(NU):
                    g, m = u // C, u % C
                    for c in range(C):
                        last_mm = nc.tensor.matmul(k.psum[:, u, :], w[:, 2 * g + 1, c, m * P:(m + 1) * P],
                                                   cell[:, 0, c, :], start=False, stop=(c == C - 1))
                    last_mm.then_inc(g_ready, 1)
                if not last:
                    transposes(n + 1)
                pe.wait_ge(c_ready, n * 2 * C + 2 * C)
                for i in range(NO):
                    t, pair = i // 2, i % 2
                    if not last:
                        pe.wait_ge(t_free, 2 + (n + 2) * NT)
                    pe.wait_ge(pre_done, n * NO + i + 1)
                    for t2 in range(2):
                        tile = slice((2 * pair + t2) * P, (2 * pair + t2 + 1) * P)
                        out = k.psum[:, 6 + pair, t2 * D:(t2 + 1) * D]
                        for c in range(C):
                            nc.tensor.matmul(out, xT[:, r, t, c, tile], w[:, 6, c, :], start=(c == 0), stop=False)
                        for c in range(C):
                            last_mm = nc.tensor.matmul(out, cell[:, 1, c, tile], w[:, 7, c, :],
                                                       start=False, stop=(c == C - 1))
                    last_mm.then_inc(o_ready, 1)

            looped(pe, NBK, blockwise)

        @block.scalar
        def _(act):
            act.sem_inc(t_free, 2)
            act.sem_inc(g_done, NU)

            def chunks(n, r):
                for i in range(NT):
                    act.wait_ge(t_ready, n * NT + i + 1)
                    nc.scalar.copy(xT[:, r, i // C, i % C, :], k.psum[:, 6 + i % C, :]).then_inc(t_free, 1)

            chunks(0, 0)
            act.wait_ge(s_b0, 2)

            def blockwise(n, r, last):
                for s in range(2):
                    bias = b if s else b0
                    for u in range(NU):
                        g, m = u // C, u % C
                        act.wait_ge(g_ready, n * 2 * NU + s * NU + u + 1)
                        nc.scalar.activation(gates[:, s, g, m, :], k.psum[:, u, :],
                                             ACT.Tanh if g == 2 else ACT.Sigmoid,
                                             bias=bias[:, g, m:m + 1]).then_inc(g_done, 1)
                if not last:
                    chunks(n + 1, 1 - r)
                for i in range(NO):
                    act.wait_ge(pre_done, 2 + n * NO + i + 1)
                    act.wait_ge(x_done, n * NO + i + 1)
                    nc.scalar.activation(th[:, i % 2, :], pre[:, i % 2, :], ACT.Tanh).then_inc(th_done, 1)

            looped(act, NBK, blockwise)

        @block.vector
        def _(dve):
            dve.sem_inc(pre_done, 2)
            dve.sem_inc(x_done, 2)
            dve.wait_ge(s_w, 16 * 3)

            def normalize(n):
                for t in range(2):
                    ln.dve_stats(dve, n * 2 + t, t, n * TB + t * (TT // NB))
                for t in range(2):
                    ln.dve_apply(dve, n * 2 + t, t, n * TB + t * (TT // NB))

            normalize(0)
            dve.wait_ge(s_b0, 1)
            nc.vector.tensor_tensor(b0, k.psum[:, 5, 0:NU].rearrange("p (g c) -> p g c", g=3), b[:, 0:3, :],
                                    ALU.add).then_inc(s_b0, 1)

            def state(n, s):
                base = n * 3 * C + (C if s else 0)
                for m in range(C):
                    dve.wait_ge(g_done, NU + n * 2 * NU + s * NU + 2 * C + m + 1)
                    nc.vector.tensor_tensor(ig[:, m, :], gates[:, s, 1, m, :], gates[:, s, 2, m, :],
                                            ALU.mult).then_inc(ig_done, 1)
                    if s:
                        nc.vector.tensor_tensor(fc[:, m, :], gates[:, s, 0, m, :], cell[:, 0, m, :],
                                                ALU.mult).then_inc(ig_done, 1)
                        dve.wait_ge(ig_done, base + 2 * m + 2)
                        nc.vector.tensor_tensor(cell[:, 1, m, :], fc[:, m, :], ig[:, m, :], ALU.add).then_inc(c_ready, 1)
                    else:
                        dve.wait_ge(ig_done, base + m + 1)
                        nc.vector.scalar_tensor_tensor(cell[:, 0, m, :], gates[:, s, 0, m, :], b[:, 3, m:m + 1],
                                                       ig[:, m, :], ALU.mult, ALU.add).then_inc(c_ready, 1)

            def update(n, i):
                t, pair = i // 2, i % 2
                dve.wait_ge(th_done, n * NO + i + 1)
                tiles = k.X[:, bass.ds(n * TB + t * (TT // NB) + 2 * pair, 2), :]
                nc.vector.scalar_tensor_tensor(tiles, th[:, i % 2, :].rearrange("p (t n) -> p t n", t=2), 0.5, tiles,
                                               ALU.mult, ALU.add).then_inc(x_done, 1)

            def blockwise(n, r, last):
                state(n, 0)
                if not last:
                    normalize(n + 1)
                dve.wait_ge(c_ready, n * 2 * C + C)
                state(n, 1)
                for i in range(NO):
                    dve.wait_ge(o_ready, n * NO + i + 1)
                    nc.vector.tensor_tensor(pre[:, i % 2, :].rearrange("p (t n) -> p t n", t=2),
                                            k.psum[:, 6 + i % 2, :].rearrange("p (t n) -> p t n", t=2),
                                            bo.unsqueeze(1).to_broadcast([P, 2, D]), ALU.add).then_inc(pre_done, 1)
                    if i:
                        update(n, i - 1)
                update(n, NO - 1)

            looped(dve, NBK, blockwise)




def store_stage(k, ctx):
    nc, io = k.nc, k.io
    s_out = k.semaphore("s_out")
    with nc.Block() as block:
        @block.sync
        def _(sp):
            o_t = io["out"].rearrange("b (t p) d -> p (b t) d", p=P)
            for i in range(4):
                n = TT // 4
                sp.dma_start(o_t[:, i * n:(i + 1) * n, :], k.X[:, i * n:(i + 1) * n, :]).then_inc(s_out, 16)
            sp.wait_ge(s_out, 16 * 4)


def program(nc, io, stages):
    with ExitStack() as ctx:
        k = alloc(nc, ctx, io)
        alloc_attention(k, ctx)
        load_stage(k, ctx)
        k.free_semaphores()
        for st in stages:
            st(k, ctx)
            k.free_semaphores()
        store_stage(k, ctx)


def moe(run):
    return lambda k, ctx: moe_stage(k, ctx, run)


def attention(causal):
    def stage(k, ctx):
        with ExitStack() as local:
            alloc_scratch(k, local)
            qkv_stage(k, ctx, causal)
            k.free_semaphores()
            heads_stage(k, ctx, causal)
            k.free_semaphores()
            project_stage(k, ctx, causal)
    return stage


def lstm(run):
    def stage(k, ctx):
        with ExitStack() as local:
            alloc_scratch(k, local)
            lstm_stage(k, ctx, run)
    return stage


STAGES = [moe(0), attention(False), moe(1), lstm(0), attention(True), lstm(1)]


def _tables():
    f = np.float32
    inv = (f(1.0) / f(10000.0) ** (np.arange(0, DH, 2, dtype=f) / f(DH))).astype(f)
    ang = np.outer(np.arange(S, dtype=f), inv).astype(f)
    cos, sin = np.cos(ang).astype(f), np.sin(ang).astype(f)
    pair = (np.arange(P) % DH) // 2
    sign = np.where(np.arange(P) % 2 == 0, f(-1), f(1))[:, None]
    rope = np.stack([cos.T[pair], sign * sin.T[pair]], axis=1).astype(f)
    r, c = np.arange(P)[:, None], np.arange(SKEW)[None, :]
    mask = np.where(c - REL > r, f(NEG), f(0)).astype(f)
    hm = (np.arange(P)[:, None] // DH == np.arange(HC)[None, :]).astype(f)
    spread = np.ascontiguousarray(hm.T)
    jm = (np.arange(P)[:, None] // REL == np.arange(GROUP)[None, :]).astype(f)
    return {"rope": rope, "bias0": mask, "hmask": hm, "jmask": jm, "spread": spread}


def _feature_major(ws):
    w = np.stack([np.asarray(x).T for x in ws])
    n, i, o = w.shape
    return np.ascontiguousarray(w.reshape(n, C, P, o).transpose(2, 0, 1, 3).reshape(P, n * C * o))


def kernel(**inputs):
    import numpy as _np
    import concourse.bacc as _bacc
    from concourse import mybir as _mybir
    from concourse.bass_utils import run_bass_kernel_spmd as _run

    a = {n: _np.asarray(v) for n, v in inputs.items()}
    arrays = {"x": a["L0_attn_x"]}
    moe = []
    for e in range(E):
        moe += [a["L0_ffn_ew1"][e], a["L0_ffn_ew3"][e], a["L0_ffn_ew2"][e]]
    moe += [a["L0_ffn_fc1"], a["L0_ffn_fc2"], a["L0_ffn_fc3"]]
    arrays["moe_w"] = _feature_major(moe)
    arrays["gwT"] = _np.ascontiguousarray(a["L0_ffn_gate_w"].T.reshape(C, P, E).transpose(1, 0, 2))
    arrays["gb"] = a["L0_ffn_gate_b"].reshape(E, 1)
    arrays["attn0_w"] = _feature_major([a["L0_attn_Wq"], a["L0_attn_Wk"], a["L0_attn_Wv"], a["L0_attn_Wff"]])
    arrays["bff"] = a["L0_attn_bff"].reshape(1, D)
    swap = _np.arange(D).reshape(D // 2, 2)[:, ::-1].reshape(D)
    arrays["attn1_w"] = _feature_major([a["L1_attn_w_q"], a["L1_attn_w_k"], a["L1_attn_w_v"], a["L1_attn_w_o"],
                                        a["L1_attn_w_q"][swap], a["L1_attn_w_k"][swap]])
    arrays["rel"] = a["L1_attn_rel_emb"]
    arrays["relT"] = _np.tile(a["L1_attn_rel_emb"][:1 + REL].T, (HC, 1))
    arrays["lstm_w"] = _feature_major([a["L1_ffn_" + n] for n in ("wf", "uf", "wi", "ui", "wc", "uc", "wo", "uo")])
    arrays["lstm_b"] = _np.ascontiguousarray(
        _np.stack([a["L1_ffn_" + n] for n in ("bf", "bi", "bc", "in_c")]).reshape(4, C, P).transpose(2, 0, 1))
    arrays["bo"] = a["L1_ffn_bo"].reshape(1, D)
    arrays.update(_tables())
    arrays["ident"] = _np.eye(P, dtype=_np.float32)
    arrays["tie"] = _np.tile(_np.tril(_np.ones((E, E), _np.float32), -1).reshape(1, E * E), (P, 1))

    nc = _bacc.Bacc("TRN2", target_bir_lowering=False, num_devices=1)
    maps, io = {}, {}
    for name, v in arrays.items():
        v = _np.ascontiguousarray(v)
        maps[f"in_{name}"] = v
        io[name] = nc.dram_tensor(f"in_{name}", v.shape, _mybir.dt.from_np(v.dtype), kind="ExternalInput").ap()
    io["out"] = nc.dram_tensor("out_0", (NB, S, D), _mybir.dt.float32, kind="ExternalOutput").ap()
    program(nc, io, STAGES)
    r = _run(nc, [maps], core_ids=[0])
    return r.results[0]["out_0"]
```
